# Optimizing a Trainium2 kernel written in Bass

```python
import numpy as np
import jax
import jax.numpy as jnp

def _softmax(x, axis=-1):
    return jax.nn.softmax(x, axis=axis)

def _gelu(x):
    return jax.nn.gelu(x, approximate=True)

def _silu(x):
    return jax.nn.silu(x)

def _sigmoid(x):
    return jax.nn.sigmoid(x)

def _layernorm(x, axis=-1, eps=1e-05):
    m = jnp.mean(x, axis=axis, keepdims=True)
    v = jnp.var(x, axis=axis, keepdims=True)
    return (x - m) / jnp.sqrt(v + eps)

def _scatter_add(tgt, idx, src, axis=0):
    return tgt.at[idx].add(src)

def _segment_sum(src, seg, n):
    return jax.ops.segment_sum(src, seg, n)
kernel_name = 'mk_conv_seq_d2_conv_nhwc192_r4_365d18'

def setup_inputs(seed: int=0):
    np.random.seed(seed)
    _w = jnp.asarray

    def _rec_inputs():
        import jax
        import jax.numpy as jnp
        _gk = jax.random.key(seed)
        x = -0.000357 + 1 * jax.random.normal(jax.random.fold_in(_gk, 1), (32, 56, 56, 48), jnp.float32)
        return x
    x = _rec_inputs()

    def _L0_conv_setup():
        import jax, jax.numpy as jnp
        import numpy as np
        DIM = 48
        H = 56
        W = 56
        HEADS = 6
        WIN = 7
        SHIFT = 3
        HD = DIM // HEADS
        N = WIN * WIN

        def _rel_pos_index():
            coords = np.stack(np.meshgrid(np.arange(WIN), np.arange(WIN), indexing='ij'))
            cf = coords.reshape(2, -1)
            rel = (cf[:, :, None] - cf[:, None, :]).transpose(1, 2, 0)
            rel[:, :, 0] += WIN - 1
            rel[:, :, 1] += WIN - 1
            rel[:, :, 0] *= 2 * WIN - 1
            return rel.sum(-1)

        def _attn_mask():
            img = np.zeros((1, H, W, 1), dtype=np.float32)
            slices = (slice(0, -WIN), slice(-WIN, -SHIFT), slice(-SHIFT, None))
            cnt = 0
            for hs in slices:
                for ws in slices:
                    img[:, hs, ws, :] = cnt
                    cnt += 1
            mw = img.reshape(1, H // WIN, WIN, W // WIN, WIN, 1).transpose(0, 1, 3, 2, 4, 5).reshape(-1, N)
            am = mw[:, None, :] - mw[:, :, None]
            return np.where(am != 0, np.float32(-100.0), np.float32(0.0))
        REL_IDX = _rel_pos_index().reshape(-1)
        ATTN_MASK = _attn_mask()

        def _layernorm(x, w, b):
            m = x.mean(-1, keepdims=True)
            v = ((x - m) ** 2).mean(-1, keepdims=True)
            return (x - m) * jax.lax.rsqrt(v + 1e-05) * w + b
        key = jax.random.key(seed)
        ks = jax.random.split(key, 8)
        s = 0.02
        return {'x': jax.random.normal(ks[0], (32, H, W, DIM), jnp.float32), 'norm1_w': jnp.ones((DIM,), jnp.float32), 'norm1_b': jnp.zeros((DIM,), jnp.float32), 'qkv_w': jax.random.normal(ks[1], (DIM, 3 * DIM), jnp.float32) * s, 'qkv_b': jnp.zeros((3 * DIM,), jnp.float32), 'proj_w': jax.random.normal(ks[2], (DIM, DIM), jnp.float32) * s, 'proj_b': jnp.zeros((DIM,), jnp.float32), 'rpb_table': jax.random.normal(ks[3], ((2 * WIN - 1) ** 2, HEADS), jnp.float32) * s, 'norm2_w': jnp.ones((DIM,), jnp.float32), 'norm2_b': jnp.zeros((DIM,), jnp.float32), 'fc1_w': jax.random.normal(ks[4], (DIM, 4 * DIM), jnp.float32) * s, 'fc1_b': jnp.zeros((4 * DIM,), jnp.float32), 'fc2_w': jax.random.normal(ks[5], (4 * DIM, DIM), jnp.float32) * s, 'fc2_b': jnp.zeros((DIM,), jnp.float32)}
    _L0_conv_all = _L0_conv_setup()
    _L0_conv_in = {k: v for k, v in _L0_conv_all.items() if k in ('norm1_w', 'norm1_b', 'qkv_w', 'qkv_b', 'proj_w', 'proj_b', 'rpb_table', 'norm2_w', 'norm2_b', 'fc1_w', 'fc1_b', 'fc2_w', 'fc2_b')}
    del _L0_conv_all

    def _L1_conv_setup():
        import jax, jax.numpy as jnp
        import numpy as np
        B, H, W_IMG, C = (32, 56, 56, 48)
        HEADS, WIN, SHIFT = (6, 7, 3)
        HIDDEN = 4 * C
        N = WIN * WIN
        NEG = -1000000000.0

        def _rel_index_np():
            coords = np.stack(np.meshgrid(np.arange(WIN), np.arange(WIN), indexing='ij'))
            coords = coords.reshape(2, -1)
            rel = coords[:, :, None] - coords[:, None, :]
            rel = rel.transpose(1, 2, 0) + (WIN - 1)
            return (rel[..., 0] * (2 * WIN - 1) + rel[..., 1]).astype(np.int32)

        def _shift_mask_np():
            img = np.zeros((H, W_IMG), np.int32)
            cnt = 0
            sl = (slice(0, -WIN), slice(-WIN, -SHIFT), slice(-SHIFT, None))
            for hs in sl:
                for ws in sl:
                    img[hs, ws] = cnt
                    cnt += 1
            m = img.reshape(H // WIN, WIN, W_IMG // WIN, WIN).transpose(0, 2, 1, 3).reshape(-1, N)
            diff = m[:, None, :] != m[:, :, None]
            return np.where(diff, NEG, 0.0).astype(np.float32)
        _SHIFT_MASK = _shift_mask_np()

        def window_partition(x):
            b, h, w, c = x.shape
            x = x.reshape(b, h // WIN, WIN, w // WIN, WIN, c).transpose(0, 1, 3, 2, 4, 5)
            return x.reshape(-1, N, c)

        def window_reverse(win, b, h, w):
            c = win.shape[-1]
            x = win.reshape(b, h // WIN, w // WIN, WIN, WIN, c).transpose(0, 1, 3, 2, 4, 5)
            return x.reshape(b, h, w, c)

        def layer_norm(x, g, b):
            mu = x.mean(-1, keepdims=True)
            var = x.var(-1, keepdims=True)
            return (x - mu) * jax.lax.rsqrt(var + 1e-05) * g + b

        def window_attention(x, qkv_w, qkv_b, proj_w, proj_b, rel_table, rel_index, shifted):
            b, h, w, c = x.shape
            if shifted:
                x = jnp.roll(x, (-SHIFT, -SHIFT), axis=(1, 2))
            win = window_partition(x)
            dh = c // HEADS
            qkv = win @ qkv_w + qkv_b
            q, k, v = jnp.split(qkv, 3, axis=-1)

            def to_heads(t):
                return t.reshape(-1, N, HEADS, dh).transpose(0, 2, 1, 3)
            q = to_heads(q) * dh ** (-0.5)
            k, v = (to_heads(k), to_heads(v))
            attn = jnp.einsum('bhnd,bhmd->bhnm', q, k)
            bias = rel_table[rel_index]
            attn = attn + bias.transpose(2, 0, 1)[None]
            if shifted:
                mask = jnp.asarray(_SHIFT_MASK)
                nW = mask.shape[0]
                attn = attn.reshape(b, nW, HEADS, N, N) + mask[None, :, None]
                attn = attn.reshape(-1, HEADS, N, N)
            attn = jax.nn.softmax(attn, axis=-1)
            out = jnp.einsum('bhnm,bhmd->bhnd', attn, v).transpose(0, 2, 1, 3).reshape(-1, N, c)
            out = out @ proj_w + proj_b
            x = window_reverse(out, b, h, w)
            if shifted:
                x = jnp.roll(x, (SHIFT, SHIFT), axis=(1, 2))
            return x

        def mlp(x, w1, b1, w2, b2):
            return jax.nn.gelu(x @ w1 + b1) @ w2 + b2
        key = jax.random.key(seed)
        ks = jax.random.split(key, 8)
        s = 0.02
        return {'image': jax.random.normal(ks[0], (B, H, W_IMG, C), jnp.float32), 'ln1_g': jnp.ones((C,), jnp.float32), 'ln1_b': jnp.zeros((C,), jnp.float32), 'ln2_g': jnp.ones((C,), jnp.float32), 'ln2_b': jnp.zeros((C,), jnp.float32), 'w_qkv_w': jax.random.normal(ks[1], (C, 3 * C), jnp.float32) * s, 'w_qkv_b': jnp.zeros((3 * C,), jnp.float32), 'w_proj_w': jax.random.normal(ks[2], (C, C), jnp.float32) * s, 'w_proj_b': jnp.zeros((C,), jnp.float32), 'w_rel': jax.random.normal(ks[3], ((2 * WIN - 1) ** 2, HEADS), jnp.float32) * s, 's_qkv_w': jax.random.normal(ks[4], (C, 3 * C), jnp.float32) * s, 's_qkv_b': jnp.zeros((3 * C,), jnp.float32), 's_proj_w': jax.random.normal(ks[5], (C, C), jnp.float32) * s, 's_proj_b': jnp.zeros((C,), jnp.float32), 's_rel': jax.random.normal(ks[6], ((2 * WIN - 1) ** 2, HEADS), jnp.float32) * s, 'mlp_w1': jax.random.normal(ks[7], (C, HIDDEN), jnp.float32) * s, 'mlp_b1': jnp.zeros((HIDDEN,), jnp.float32), 'mlp_w2': jax.random.normal(jax.random.fold_in(key, 99), (HIDDEN, C), jnp.float32) * s, 'mlp_b2': jnp.zeros((C,), jnp.float32), 'rel_index': jnp.asarray(_rel_index_np())}
    _L1_conv_all = _L1_conv_setup()
    _L1_conv_in = {k: v for k, v in _L1_conv_all.items() if k in ('ln1_g', 'ln1_b', 'ln2_g', 'ln2_b', 'w_qkv_w', 'w_qkv_b', 'w_proj_w', 'w_proj_b', 'w_rel', 's_qkv_w', 's_qkv_b', 's_proj_w', 's_proj_b', 's_rel', 'mlp_w1', 'mlp_b1', 'mlp_w2', 'mlp_b2', 'rel_index')}
    del _L1_conv_all
    return {'x': x, 'L0_conv_norm1_w': _L0_conv_in['norm1_w'], 'L0_conv_norm1_b': _L0_conv_in['norm1_b'], 'L0_conv_qkv_w': _L0_conv_in['qkv_w'], 'L0_conv_qkv_b': _L0_conv_in['qkv_b'], 'L0_conv_proj_w': _L0_conv_in['proj_w'], 'L0_conv_proj_b': _L0_conv_in['proj_b'], 'L0_conv_rpb_table': _L0_conv_in['rpb_table'], 'L0_conv_norm2_w': _L0_conv_in['norm2_w'], 'L0_conv_norm2_b': _L0_conv_in['norm2_b'], 'L0_conv_fc1_w': _L0_conv_in['fc1_w'], 'L0_conv_fc1_b': _L0_conv_in['fc1_b'], 'L0_conv_fc2_w': _L0_conv_in['fc2_w'], 'L0_conv_fc2_b': _L0_conv_in['fc2_b'], 'L1_conv_ln1_g': _L1_conv_in['ln1_g'], 'L1_conv_ln1_b': _L1_conv_in['ln1_b'], 'L1_conv_ln2_g': _L1_conv_in['ln2_g'], 'L1_conv_ln2_b': _L1_conv_in['ln2_b'], 'L1_conv_w_qkv_w': _L1_conv_in['w_qkv_w'], 'L1_conv_w_qkv_b': _L1_conv_in['w_qkv_b'], 'L1_conv_w_proj_w': _L1_conv_in['w_proj_w'], 'L1_conv_w_proj_b': _L1_conv_in['w_proj_b'], 'L1_conv_w_rel': _L1_conv_in['w_rel'], 'L1_conv_s_qkv_w': _L1_conv_in['s_qkv_w'], 'L1_conv_s_qkv_b': _L1_conv_in['s_qkv_b'], 'L1_conv_s_proj_w': _L1_conv_in['s_proj_w'], 'L1_conv_s_proj_b': _L1_conv_in['s_proj_b'], 'L1_conv_s_rel': _L1_conv_in['s_rel'], 'L1_conv_mlp_w1': _L1_conv_in['mlp_w1'], 'L1_conv_mlp_b1': _L1_conv_in['mlp_b1'], 'L1_conv_mlp_w2': _L1_conv_in['mlp_w2'], 'L1_conv_mlp_b2': _L1_conv_in['mlp_b2'], 'L1_conv_rel_index': _L1_conv_in['rel_index']}

def reference(x, L0_conv_norm1_w, L0_conv_norm1_b, L0_conv_qkv_w, L0_conv_qkv_b, L0_conv_proj_w, L0_conv_proj_b, L0_conv_rpb_table, L0_conv_norm2_w, L0_conv_norm2_b, L0_conv_fc1_w, L0_conv_fc1_b, L0_conv_fc2_w, L0_conv_fc2_b, L1_conv_ln1_g, L1_conv_ln1_b, L1_conv_ln2_g, L1_conv_ln2_b, L1_conv_w_qkv_w, L1_conv_w_qkv_b, L1_conv_w_proj_w, L1_conv_w_proj_b, L1_conv_w_rel, L1_conv_s_qkv_w, L1_conv_s_qkv_b, L1_conv_s_proj_w, L1_conv_s_proj_b, L1_conv_s_rel, L1_conv_mlp_w1, L1_conv_mlp_b1, L1_conv_mlp_w2, L1_conv_mlp_b2, L1_conv_rel_index):
    import jax
    import jax.numpy as jnp

    def _L0_conv_ref(x, norm1_w, norm1_b, qkv_w, qkv_b, proj_w, proj_b, rpb_table, norm2_w, norm2_b, fc1_w, fc1_b, fc2_w, fc2_b):
        import jax, jax.numpy as jnp
        import numpy as np
        DIM = 48
        H = 56
        W = 56
        HEADS = 6
        WIN = 7
        SHIFT = 3
        HD = DIM // HEADS
        N = WIN * WIN

        def _rel_pos_index():
            coords = np.stack(np.meshgrid(np.arange(WIN), np.arange(WIN), indexing='ij'))
            cf = coords.reshape(2, -1)
            rel = (cf[:, :, None] - cf[:, None, :]).transpose(1, 2, 0)
            rel[:, :, 0] += WIN - 1
            rel[:, :, 1] += WIN - 1
            rel[:, :, 0] *= 2 * WIN - 1
            return rel.sum(-1)

        def _attn_mask():
            img = np.zeros((1, H, W, 1), dtype=np.float32)
            slices = (slice(0, -WIN), slice(-WIN, -SHIFT), slice(-SHIFT, None))
            cnt = 0
            for hs in slices:
                for ws in slices:
                    img[:, hs, ws, :] = cnt
                    cnt += 1
            mw = img.reshape(1, H // WIN, WIN, W // WIN, WIN, 1).transpose(0, 1, 3, 2, 4, 5).reshape(-1, N)
            am = mw[:, None, :] - mw[:, :, None]
            return np.where(am != 0, np.float32(-100.0), np.float32(0.0))
        REL_IDX = _rel_pos_index().reshape(-1)
        ATTN_MASK = _attn_mask()

        def _layernorm(x, w, b):
            m = x.mean(-1, keepdims=True)
            v = ((x - m) ** 2).mean(-1, keepdims=True)
            return (x - m) * jax.lax.rsqrt(v + 1e-05) * w + b
        B = x.shape[0]
        shortcut = x
        xn = _layernorm(x, norm1_w, norm1_b)
        xs = jnp.roll(xn, (-SHIFT, -SHIFT), axis=(1, 2))
        xw = xs.reshape(B, H // WIN, WIN, W // WIN, WIN, DIM)
        xw = xw.transpose(0, 1, 3, 2, 4, 5).reshape(-1, N, DIM)
        qkv = (xw @ qkv_w + qkv_b).reshape(-1, N, 3, HEADS, HD).transpose(2, 0, 3, 1, 4)
        q, k, v = (qkv[0], qkv[1], qkv[2])
        scale = HD ** (-0.5)
        attn = jnp.einsum('bhnd,bhmd->bhnm', q * scale, k)
        bias = rpb_table[REL_IDX].reshape(N, N, HEADS).transpose(2, 0, 1)
        attn = attn + bias[None]
        mask = jnp.asarray(ATTN_MASK)
        nW = mask.shape[0]
        attn = attn.reshape(-1, nW, HEADS, N, N) + mask[None, :, None]
        attn = jax.nn.softmax(attn.reshape(-1, HEADS, N, N), axis=-1)
        out = jnp.einsum('bhnm,bhmd->bhnd', attn, v).transpose(0, 2, 1, 3).reshape(-1, N, DIM)
        out = out @ proj_w + proj_b
        out = out.reshape(B, H // WIN, W // WIN, WIN, WIN, DIM)
        out = out.transpose(0, 1, 3, 2, 4, 5).reshape(B, H, W, DIM)
        out = jnp.roll(out, (SHIFT, SHIFT), axis=(1, 2))
        x = shortcut + out
        xn2 = _layernorm(x, norm2_w, norm2_b)
        h = jax.nn.gelu(xn2 @ fc1_w + fc1_b, approximate=False)
        return x + (h @ fc2_w + fc2_b)

    def _L1_conv_ref(image, ln1_g, ln1_b, ln2_g, ln2_b, w_qkv_w, w_qkv_b, w_proj_w, w_proj_b, w_rel, s_qkv_w, s_qkv_b, s_proj_w, s_proj_b, s_rel, mlp_w1, mlp_b1, mlp_w2, mlp_b2, rel_index):
        import jax, jax.numpy as jnp
        import numpy as np
        B, H, W_IMG, C = (32, 56, 56, 48)
        HEADS, WIN, SHIFT = (6, 7, 3)
        HIDDEN = 4 * C
        N = WIN * WIN
        NEG = -1000000000.0

        def _rel_index_np():
            coords = np.stack(np.meshgrid(np.arange(WIN), np.arange(WIN), indexing='ij'))
            coords = coords.reshape(2, -1)
            rel = coords[:, :, None] - coords[:, None, :]
            rel = rel.transpose(1, 2, 0) + (WIN - 1)
            return (rel[..., 0] * (2 * WIN - 1) + rel[..., 1]).astype(np.int32)

        def _shift_mask_np():
            img = np.zeros((H, W_IMG), np.int32)
            cnt = 0
            sl = (slice(0, -WIN), slice(-WIN, -SHIFT), slice(-SHIFT, None))
            for hs in sl:
                for ws in sl:
                    img[hs, ws] = cnt
                    cnt += 1
            m = img.reshape(H // WIN, WIN, W_IMG // WIN, WIN).transpose(0, 2, 1, 3).reshape(-1, N)
            diff = m[:, None, :] != m[:, :, None]
            return np.where(diff, NEG, 0.0).astype(np.float32)
        _SHIFT_MASK = _shift_mask_np()

        def window_partition(x):
            b, h, w, c = x.shape
            x = x.reshape(b, h // WIN, WIN, w // WIN, WIN, c).transpose(0, 1, 3, 2, 4, 5)
            return x.reshape(-1, N, c)

        def window_reverse(win, b, h, w):
            c = win.shape[-1]
            x = win.reshape(b, h // WIN, w // WIN, WIN, WIN, c).transpose(0, 1, 3, 2, 4, 5)
            return x.reshape(b, h, w, c)

        def layer_norm(x, g, b):
            mu = x.mean(-1, keepdims=True)
            var = x.var(-1, keepdims=True)
            return (x - mu) * jax.lax.rsqrt(var + 1e-05) * g + b

        def window_attention(x, qkv_w, qkv_b, proj_w, proj_b, rel_table, rel_index, shifted):
            b, h, w, c = x.shape
            if shifted:
                x = jnp.roll(x, (-SHIFT, -SHIFT), axis=(1, 2))
            win = window_partition(x)
            dh = c // HEADS
            qkv = win @ qkv_w + qkv_b
            q, k, v = jnp.split(qkv, 3, axis=-1)

            def to_heads(t):
                return t.reshape(-1, N, HEADS, dh).transpose(0, 2, 1, 3)
            q = to_heads(q) * dh ** (-0.5)
            k, v = (to_heads(k), to_heads(v))
            attn = jnp.einsum('bhnd,bhmd->bhnm', q, k)
            bias = rel_table[rel_index]
            attn = attn + bias.transpose(2, 0, 1)[None]
            if shifted:
                mask = jnp.asarray(_SHIFT_MASK)
                nW = mask.shape[0]
                attn = attn.reshape(b, nW, HEADS, N, N) + mask[None, :, None]
                attn = attn.reshape(-1, HEADS, N, N)
            attn = jax.nn.softmax(attn, axis=-1)
            out = jnp.einsum('bhnm,bhmd->bhnd', attn, v).transpose(0, 2, 1, 3).reshape(-1, N, c)
            out = out @ proj_w + proj_b
            x = window_reverse(out, b, h, w)
            if shifted:
                x = jnp.roll(x, (SHIFT, SHIFT), axis=(1, 2))
            return x

        def mlp(x, w1, b1, w2, b2):
            return jax.nn.gelu(x @ w1 + b1) @ w2 + b2
        x = image
        x = x + window_attention(layer_norm(x, ln1_g, ln1_b), w_qkv_w, w_qkv_b, w_proj_w, w_proj_b, w_rel, rel_index, False)
        x = x + mlp(layer_norm(x, ln2_g, ln2_b), mlp_w1, mlp_b1, mlp_w2, mlp_b2)
        x = x + window_attention(layer_norm(x, ln1_g, ln1_b), s_qkv_w, s_qkv_b, s_proj_w, s_proj_b, s_rel, rel_index, True)
        x = x + mlp(layer_norm(x, ln2_g, ln2_b), mlp_w1, mlp_b1, mlp_w2, mlp_b2)
        return x

    def _gn(v, G=32, eps=1e-05):
        B_, H_, W_, C_ = v.shape
        g = v.reshape(B_, H_, W_, G, C_ // G)
        m = jnp.mean(g, axis=(1, 2, 4), keepdims=True)
        s = jnp.var(g, axis=(1, 2, 4), keepdims=True)
        return ((g - m) / jnp.sqrt(s + eps)).reshape(v.shape)

    def _ln_c(v, eps=1e-06):
        m = jnp.mean(v, axis=-1, keepdims=True)
        s = jnp.var(v, axis=-1, keepdims=True)
        return (v - m) / jnp.sqrt(s + eps)

    def _ln_t(v, eps=1e-05):
        m = jnp.mean(v, axis=-1, keepdims=True)
        s = jnp.var(v, axis=-1, keepdims=True)
        return (v - m) / jnp.sqrt(s + eps)

    def _to_tokens(v):
        B_, H_, W_, C_ = v.shape
        return v.reshape(B_, H_ * W_, C_)

    def _from_tokens(t, like):
        return t.reshape(like.shape)
    x = _L0_conv_ref(x, L0_conv_norm1_w, L0_conv_norm1_b, L0_conv_qkv_w, L0_conv_qkv_b, L0_conv_proj_w, L0_conv_proj_b, L0_conv_rpb_table, L0_conv_norm2_w, L0_conv_norm2_b, L0_conv_fc1_w, L0_conv_fc1_b, L0_conv_fc2_w, L0_conv_fc2_b)
    x = _L1_conv_ref(x, L1_conv_ln1_g, L1_conv_ln1_b, L1_conv_ln2_g, L1_conv_ln2_b, L1_conv_w_qkv_w, L1_conv_w_qkv_b, L1_conv_w_proj_w, L1_conv_w_proj_b, L1_conv_w_rel, L1_conv_s_qkv_w, L1_conv_s_qkv_b, L1_conv_s_proj_w, L1_conv_s_proj_b, L1_conv_s_rel, L1_conv_mlp_w1, L1_conv_mlp_b1, L1_conv_mlp_w2, L1_conv_mlp_b2, L1_conv_rel_index)
    return x

_drawn_inputs = setup_inputs


def setup_inputs(seed=0):
    import zlib

    import numpy as np

    out = dict(_drawn_inputs(seed))
    spreads = {'L0_conv_norm1_w': (1.0, 0.6),
     'L0_conv_norm1_b': (0.0, 0.8),
     'L0_conv_qkv_b': (0.0, 0.734),
     'L0_conv_proj_b': (0.0, 0.1),
     'L0_conv_norm2_w': (1.0, 0.6),
     'L0_conv_norm2_b': (0.0, 2.0),
     'L0_conv_fc1_b': (0.0, 0.46),
     'L0_conv_fc2_b': (0.0, 0.1),
     'L1_conv_ln1_g': (1.0, 0.6),
     'L1_conv_ln1_b': (0.0, 0.8),
     'L1_conv_ln2_g': (1.0, 0.6),
     'L1_conv_ln2_b': (0.0, 2.0),
     'L1_conv_w_qkv_b': (0.0, 0.636),
     'L1_conv_w_proj_b': (0.0, 0.1),
     'L1_conv_s_qkv_b': (0.0, 0.497),
     'L1_conv_s_proj_b': (0.0, 0.1),
     'L1_conv_mlp_b1': (0.0, 0.384),
     'L1_conv_mlp_b2': (0.0, 0.1)}
    factors = {'L0_conv_qkv_w': 8.0,
     'L0_conv_proj_w': 5.615,
     'L0_conv_rpb_table': 8.0,
     'L1_conv_w_qkv_w': 8.0,
     'L1_conv_w_proj_w': 4.079,
     'L1_conv_w_rel': 33.672,
     'L1_conv_s_qkv_w': 8.0,
     'L1_conv_s_proj_w': 3.523,
     'L1_conv_s_rel': 42.233}
    for name, (base, spread) in spreads.items():
        noise = np.random.default_rng([zlib.crc32(name.encode()), seed]).standard_normal(out[name].shape)
        drawn = base * np.exp(spread * noise) if base else spread * noise
        out[name] = jnp.asarray(drawn.astype(out[name].dtype))
    for name, factor in factors.items():
        out[name] = (out[name] * factor).astype(out[name].dtype)
    return out
```

```python
from contextlib import ExitStack

import numpy as np

import concourse.bass as bass
from concourse import mybir

B, H, W, C = 32, 56, 56, 48
HEADS, WIN, SHIFT = 6, 7, 3
D = C // HEADS
N = WIN * WIN
HID = 4 * C
REL = (2 * WIN - 1) ** 2
EPS = 1e-5

HI = 64
R = HI + C
M2 = HI + N
PAIRS = B // 2
G = H // WIN
STEPS = PAIRS * G
TOK = WIN * W
P = W // WIN
HN = HEADS * N
IMG = H * W
TP, TK = 98, 4
UN = 4
HP = HEADS // 2
VC = HP * C


class Step:

    def __init__(self, u, c):
        self.u, self.c = u, c

    def val(self, scale, add):
        return self.u * (UN * scale) + (self.c * scale + add)

    def uses(self, of):
        return self.u * (UN // of) + self.c // of

    def mod(self, of):
        return self.c % of


def build(nc, A, out):
    fp32, i32 = mybir.dt.float32, mybir.dt.int32
    ALU, ACT, AX = mybir.AluOpType, mybir.ActivationFunctionType, mybir.AxisListType
    ctx = ExitStack()
    with ctx:
        def sb(name, shape, dt=fp32):
            return ctx.enter_context(nc.sbuf_tensor(name, shape, dt))

        def sem(name):
            return ctx.enter_context(nc.semaphore(name))

        L0, L1 = "L0_conv_", "L1_conv_"
        mlp1 = dict(g1=L1 + "ln1_g", b1=L1 + "ln1_b", g2=L1 + "ln2_g", b2=L1 + "ln2_b",
                    w1=L1 + "mlp_w1", c1=L1 + "mlp_b1", w2=L1 + "mlp_w2", c2=L1 + "mlp_b2",
                    gelu=ACT.Gelu_apprx_tanh, index=L1 + "rel_index")
        PH = [
            dict(g1=L0 + "norm1_w", b1=L0 + "norm1_b", g2=L0 + "norm2_w", b2=L0 + "norm2_b",
                 w1=L0 + "fc1_w", c1=L0 + "fc1_b", w2=L0 + "fc2_w", c2=L0 + "fc2_b",
                 wqkv=L0 + "qkv_w", bqkv=L0 + "qkv_b", wp=L0 + "proj_w", bp=L0 + "proj_b",
                 table=L0 + "rpb_table", index="rel_const", gelu=ACT.Gelu, shift=SHIFT, neg=-100.0),
            dict(mlp1, wqkv=L1 + "w_qkv_w", bqkv=L1 + "w_qkv_b", wp=L1 + "w_proj_w",
                 bp=L1 + "w_proj_b", table=L1 + "w_rel", shift=0, neg=0.0),
            dict(mlp1, wqkv=L1 + "s_qkv_w", bqkv=L1 + "s_qkv_b", wp=L1 + "s_proj_w",
                 bp=L1 + "s_proj_b", table=L1 + "s_rel", shift=SHIFT, neg=-1e9),
        ]
        NPH = len(PH)

        scratch = [nc.dram_tensor(f"xT{k}", (PAIRS, R, IMG), fp32, kind="Internal").ap()
                   for k in range(NPH + 1)]
        x_tm = A["x"].rearrange("(P i) h w c -> P i (h w c)", i=2)\
                     .rearrange("P i (g p e) -> P g p i e", g=G, p=TP)
        o_tm = out.rearrange("(P i) h w c -> P i (h w c)", i=2)\
                  .rearrange("P i (g p e) -> P g p i e", g=G, p=TP)

        ident = sb("ident", [128, 128])
        center = sb("center", [R, R])
        mean = sb("mean", [R, R])
        headmask = sb("headmask", [R, HEADS])
        eps = sb("eps", [R, 1])
        kcol = sb("kcol", [128, 2])
        regions = sb("regions", [M2, 3, N])
        wq = sb("wq", [R, NPH, R])
        wk = sb("wk", [R, NPH, R])
        wvr = sb("wvr", [R, NPH, R])
        wv = sb("wv", [R, NPH, 2 * C])
        wp = sb("wp", [R, NPH, R])
        w1 = sb("w1", [R, NPH, 3, 128])
        w2 = sb("w2", [128, NPH, 3, R])
        GA1, BE1, GA2, BE2, BQ, BK, BV, BP, B2 = range(9)
        cols = sb("cols", [R, NPH, 9])
        b1c = sb("b1c", [128, NPH, 3])
        bias = sb("bias", [M2, NPH, 4, HN])

        Qbd = sb("Qbd", [R, 2, P, 128])
        V2 = sb("V2", [M2, 4, 2 * P, VC])
        E = sb("E", [M2, 2, P, HEADS, HI])
        oT = sb("oT", [R, P, N])

        with ExitStack() as early:
            def tmp(name, shape, dt=fp32):
                return early.enter_context(nc.sbuf_tensor(name, shape, dt))

            tm = tmp("tm", [TP, 4, 2, TK * C])
            tz = tmp("tz", [TP, 4, TK, 128])
            cm = tmp("cm", [R, 4, TOK])
            idx_i = tmp("idx_i", [128, N * N], i32)
            idx_f = tmp("idx_f", [128, N * N])
            oh_lo = tmp("oh_lo", [128, N * N])
            oh_hi = tmp("oh_hi", [128, N * N])
            tab = tmp("tab", [128, NPH, 2, HEADS])
            neg = tmp("neg", [M2, NPH, 3, N])

        xin = sb("xin", [R, 4, TOK])
        sq1 = sb("sq1", [R, TOK])
        va1 = sb("va1", [R, TOK])
        rs1 = sb("rs1", [R, TOK])
        xn1 = sb("xn1", [R, P, WIN, WIN])
        KT = sb("KT", [R, P, N])
        Kbd = sb("Kbd", [R, 2, P, HEADS, N])
        S = sb("S", [M2, P, HEADS, N])
        mx = sb("mx", [M2, P * HEADS])
        sm = sb("sm", [M2, P * HEADS])
        rs = sb("rs", [M2, 2, P * HEADS])
        ET = sb("ET", [M2, 2, HP, M2])
        x1 = sb("x1", [R, WIN, W])
        sq2 = sb("sq2", [R, TOK])
        va2 = sb("va2", [R, TOK])
        rs2 = sb("rs2", [R, TOK])
        xn2 = sb("xn2", [R, TOK])
        hT = sb("hT", [128, 3, TOK])
        xout = sb("xout", [R, 2, TOK])

        bank = [ctx.enter_context(nc.psum_tensor(f"bank{k}", [128, 512], fp32)) for k in range(8)]
        pS, pT, pO0, pO1, pA0, pA1, pD0, pD1 = bank
        pO = [pO0, pO1]

        def strided(ap, dims):
            return bass.AP(ap.tensor, ap.offset, [list(ap.ap[0])] + [list(d) for d in dims])

        zeroed = sem("zeroed")
        const_in = sem("const_in")
        par_in = sem("par_in")
        idx_in = sem("idx_in")
        onehot = sem("onehot")
        tab_mm = sem("tab_mm")
        tab_done = sem("tab_done")
        bias_mm = sem("bias_mm")
        fold = sem("fold")
        tm_in = [sem(f"tm_in{b}") for b in range(4)]
        tz_done, tr_done, cm_done = sem("tz_done"), sem("tr_done"), sem("cm_done")
        cm_out = [sem(f"cm_out{b}") for b in range(4)]
        cm_in = [sem(f"cm_in{b}") for b in range(4)]
        tr2_done, to_done = sem("tr2_done"), sem("to_done")
        to_out = [sem(f"to_out{b}") for b in range(4)]
        xin_in = [sem(f"xin_in{b}") for b in range(4)]
        out_st = [sem(f"out_st{b}") for b in range(2)]
        ctr1_mm, sq1_done, var1_mm, va1_done, rs1_done, xn1_done = (
            sem(n) for n in ("ctr1_mm", "sq1_done", "var1_mm", "va1_done", "rs1_done", "xn1_done"))
        q_mm, k_mm, v_mm = sem("q_mm"), sem("k_mm"), sem("v_mm")
        q_done, kT_done = sem("q_done"), sem("kT_done")
        kbd_done, v_done = sem("kbd_done"), sem("v_done")
        s_mm, s_done = sem("s_mm"), sem("s_done")
        mx_done, sub_done, exp_done, sum_done, rcp_done, norm_done = (
            sem(n) for n in ("mx_done", "sub_done", "exp_done", "sum_done", "rcp_done", "norm_done"))
        tr_mm, et_done = sem("tr_mm"), sem("et_done")
        pv_mm, oT_done = sem("pv_mm"), sem("oT_done")
        proj_mm, x1_done, ctr2_mm, sq2_done, var2_mm, va2_done, rs2_done, xn2_done = (
            sem(n) for n in ("proj_mm", "x1_done", "ctr2_mm", "sq2_done", "var2_mm", "va2_done",
                             "rs2_done", "xn2_done"))
        fc1_mm, gelu_done = sem("fc1_mm"), sem("gelu_done")
        fc2_mm, x2_done = sem("fc2_mm"), sem("x2_done")

        def col(t, j, v, o=0):
            return [(cols[r:r + C, t, j:j + 1], v[o:o + C].rearrange("(c a) -> c a", a=1)) for r in (0, HI)]

        def diag(tile, t, src):
            return [(tile[r:r + C, t, r:r + C], src) for r in (0, HI)]

        par = []
        for t, ph in enumerate(PH):
            wqkv, bqkv = A[ph["wqkv"]], A[ph["bqkv"]]
            for k, tile in enumerate((wq, wk, wvr)):
                par += diag(tile, t, wqkv[:, k * C:(k + 1) * C])
            par += diag(wp, t, A[ph["wp"]])
            for j, v, o in ((GA1, ph["g1"], 0), (BE1, ph["b1"], 0), (GA2, ph["g2"], 0), (BE2, ph["b2"], 0),
                            (BQ, ph["bqkv"], 0), (BK, ph["bqkv"], C), (BV, ph["bqkv"], 2 * C),
                            (BP, ph["bp"], 0), (B2, ph["c2"], 0)):
                par += col(t, j, A[v], o)
            for k, lo, r, h0, n in ((0, 0, 0, 0, 128), (1, 0, 0, 128, 64), (1, 64, HI, 0, 64), (2, 0, HI, 64, 128)):
                par.append((w1[r:r + C, t, k, lo:lo + n], A[ph["w1"]][:, h0:h0 + n]))
                par.append((w2[lo:lo + n, t, k, r:r + C], A[ph["w2"]][h0:h0 + n, :]))
                par.append((b1c[lo:lo + n, t, k:k + 1], A[ph["c1"]][h0:h0 + n].rearrange("(c a) -> c a", a=1)))
            par.append((tab[:, t, 0, :], A[ph["table"]][0:128, :]))
            par.append((tab[0:REL - 128, t, 1, :], A[ph["table"]][128:REL, :]))
        consts = [(ident[:, :], A["ident"]), (center[:, :], A["center"]), (mean[:, :], A["mean"]),
                  (headmask[:, :], A["headmask"]), (kcol[:, :], A["kcol"]),
                  (regions[0:N, :, :], A["regions"]), (regions[HI:M2, :, :], A["regions"])]
        TABLES = [("rel_const", [0]), (L1 + "rel_index", [1, 2])]
        CLEARED = [wq, wk, wvr, wp, w1, w2, cols, b1c, bias, Qbd, V2, E, oT, tz, tab, neg]

        def flat(tile):
            ap = tile[:]
            n = 1
            for d in ap.shape[1:]:
                n *= d
            return strided(ap, [[1, n]])

        block = ctx.enter_context(nc.Block())

        def sweep(eng, t, iteration):
            def steps(u, c):
                base = [Step(u, c + k) for k in (1, 0, -1, -2)]
                return base

            def peeled(i):
                it = [Step(0, i + k) if 0 <= i + k < STEPS else None for k in (1, 0, -1, -2)]
                iteration(*it)

            for i in range(-1, 2):
                peeled(i)
            full = (STEPS - 3) // UN
            with eng.Fori(0, full) as u:
                for k in range(UN):
                    iteration(*steps(u, 2 + k))
            for i in range(2 + UN * full, STEPS + 2):
                peeled(i)

        SPLIT = WIN - SHIFT

        def piece(t, k, j, part):
            s = PH[t]["shift"]
            pair, g = j.val(1, 0) // G, j.val(1, 0) % G
            if part == 0:
                return scratch[k][bass.ds(pair, 1), :, bass.ds(g * TOK + s * W, SPLIT * W)]\
                    .rearrange("a r n -> (a r) n")
            if s:
                g, at = (j.val(1, 1)) % G, 0
            else:
                at = SPLIT * W
            return scratch[k][bass.ds(pair, 1), :, bass.ds(g * TOK + at, SHIFT * W)]\
                .rearrange("a r n -> (a r) n")

        def of_step(dram, j):
            pair, g = j.val(1, 0) // G, j.val(1, 0) % G
            return dram[bass.ds(pair, 1), bass.ds(g, 1)].rearrange("a b p i e -> (a b p) i e")

        def mine(part):
            return slice(0, SPLIT * W) if part == 0 else slice(SPLIT * W, TOK)

        def global_val(t, j, scale=1, add=0):
            return j.val(scale, add + t * STEPS * scale)

        gv = global_val

        @block.sync
        def _(sp):
            for to, of in consts:
                sp.dma_start(to, of).then_inc(const_in, 16)

            def load_x(j):
                b = j.mod(4)
                if not (isinstance(j.u, int) and j.u == 0):
                    sp.wait_ge(tz_done, j.val(1, -3))
                sp.dma_start(tm[:, b], of_step(x_tm, j))\
                  .then_inc(tm_in[b], 16)

            for c in range(UN):
                load_x(Step(0, c))
            for k, (index, _) in enumerate(TABLES):
                if k:
                    sp.wait_ge(onehot, 1)
                sp.dma_start(idx_i[:, :], A[index].rearrange("(a n) -> a n", a=1).to_broadcast([128, N * N])
                             if len(A[index].shape) == 1 else
                             A[index].rearrange("(a n) m -> a (n m)", a=1).to_broadcast([128, N * N]))\
                  .then_inc(idx_in, 16)
            with sp.Fori(1, STEPS // UN) as u:
                for c in range(UN):
                    load_x(Step(u, c))
            for b in range(4):
                sp.wait_ge(cm_out[b], 16 * STEPS // 4)

            for t in range(NPH):
                if t:
                    for b in range(2):
                        sp.wait_ge(out_st[b], 32 * t * STEPS // 2)

                def load(j):
                    b = j.mod(4)
                    if not (isinstance(j.u, int) and j.c < 4):
                        sp.wait_ge(x1_done, gv(t, j, 1, -3))
                    for part in range(2):
                        sp.dma_start(xin[:, b, mine(part)], piece(t, t, j, part)).then_inc(xin_in[b], 16)

                def store(j):
                    b = j.mod(2)
                    sp.wait_ge(x2_done, gv(t, j, 1, 1))
                    for part in range(2):
                        sp.dma_start(piece(t, t + 1, j, part), xout[:, b, mine(part)]).then_inc(out_st[b], 16)

                load(Step(0, 0))

                def iteration(a, b, c, d):
                    nxt = Step(a.u, a.c + 1) if a else None
                    if nxt and (not isinstance(nxt.u, int) or nxt.c < STEPS):
                        load(nxt)
                    if d:
                        store(d)

                sweep(sp, t, iteration)

            for b in range(2):
                sp.wait_ge(out_st[b], 32 * NPH * STEPS // 2)

            def load_cm(j):
                b = j.mod(4)
                if not (isinstance(j.u, int) and j.u == 0):
                    sp.wait_ge(tr2_done, j.val(1, -3))
                sp.dma_start(cm[:, b], scratch[NPH][bass.ds(j.val(1, 0) // G, 1), :, bass.ds((j.val(1, 0) % G) * TOK, TOK)]
                             .rearrange("a r n -> (a r) n")).then_inc(cm_in[b], 16)

            for c in range(UN):
                load_cm(Step(0, c))
            with sp.Fori(1, STEPS // UN) as u:
                for c in range(UN):
                    load_cm(Step(u, c))

        @block.gpsimd
        def _(pool):
            for tile in CLEARED:
                pool.memset(flat(tile), 0.0).then_inc(zeroed, 1)
            pool.memset(eps[:, :], EPS).then_inc(zeroed, 1)

            for t in range(NPH):
                def norm(j, q):
                    b = j.mod(2)
                    pool.wait_ge(rcp_done, gv(t, j, 4, q + 1))
                    e = strided(E[:, b, 2 * q, 0, 0:1], [[HI, 2 * HEADS], [1, N]])
                    r = strided(rs[:, b, 2 * HEADS * q:2 * HEADS * q + 1], [[1, 2 * HEADS], [0, N]])
                    pool.tensor_tensor(e, e, r, ALU.mult).then_inc(norm_done, 1)

                def spread_k(j, half):
                    if half == 0:
                        pool.wait_ge(kT_done, gv(t, j, 1, 1))
                    p0 = half * P // 2
                    k = strided(KT[:, p0, 0:1], [[N, P // 2], [0, HEADS], [1, N]])
                    m = strided(headmask[:, 0:1], [[0, P // 2], [1, HEADS], [0, N]])
                    pool.tensor_tensor(Kbd[:, j.mod(2), p0:p0 + P // 2], k, m, ALU.mult).then_inc(kbd_done, 1)

                def iteration(a, b, c, d):
                    if c:
                        norm(c, 3)
                    if b:
                        norm(b, 0)
                    if b:
                        norm(b, 1)
                    if a:
                        spread_k(a, 0)
                    if b:
                        norm(b, 2)
                    if a:
                        spread_k(a, 1)

                if t == 0:
                    pool.wait_ge(const_in, 16 * len(consts))
                sweep(pool, t, iteration)

        @block.scalar
        def _(act):
            act.wait_ge(zeroed, len(CLEARED) + 1)
            for to, of in par:
                act.dma_start(to, of).then_inc(par_in, 16)

            def evac_cm(j):
                b = j.mod(4)
                act.wait_ge(tr_done, j.val(1, 1))
                if not (isinstance(j.u, int) and j.u == 0):
                    act.wait_ge(cm_out[b], j.uses(4) * 16)
                src = strided(bank[j.mod(2)][0:R, 0:1], [[1, TP], [TP, TK]])
                act.activation(strided(cm[:, b, 0:1], [[TK, TP], [1, TK]]), src, ACT.Copy).then_inc(cm_done, 1)
                act.wait_ge(cm_done, j.val(1, 1))
                act.dma_start(scratch[0][bass.ds(j.val(1, 0) // G, 1), :, bass.ds((j.val(1, 0) % G) * TOK, TOK)]
                              .rearrange("a r n -> (a r) n"), cm[:, b]).then_inc(cm_out[b], 16)

            for c in range(UN):
                evac_cm(Step(0, c))
            with act.Fori(1, STEPS // UN) as u:
                for c in range(UN):
                    evac_cm(Step(u, c))
            for b in range(4):
                act.wait_ge(cm_out[b], 16 * STEPS // 4)

            for t in range(NPH):
                gelu = PH[t]["gelu"]

                def evac_et(j, p):
                    act.wait_ge(tr_mm, gv(t, j, P, p + 1))
                    act.activation(flat3(ET[:, p % 2]), pT[0:M2, 0:HP * M2], ACT.Copy).then_inc(et_done, 1)

                def flat3(ap):
                    return strided(ap, [[1, HP * M2]])

                def evac_o(j):
                    act.wait_ge(pv_mm, gv(t, j, P, P))
                    for w in range(2):
                        r = HI * w
                        ins = act.activation(strided(oT[r:r + C, 0, 0:1], [[1, TOK]]), pO[w][0:C, 0:TOK],
                                             ACT.Identity, bias=cols[r:r + C, t, BV:BV + 1])
                    ins.then_inc(oT_done, 1)

                def square(j, mm, src, dst, done):
                    act.wait_ge(mm, gv(t, j, 1, 1))
                    act.activation(dst[:, :], src[0:R, 0:TOK], ACT.Square).then_inc(done, 1)

                def inverse_std(j, mm, src, va, rstd, va_done, done):
                    act.wait_ge(mm, gv(t, j, 1, 1))
                    act.activation(va[:, :], src[0:R, 0:TOK], ACT.Ln, bias=eps[:, 0:1]).then_inc(va_done, 1)
                    act.wait_ge(va_done, gv(t, j, 1, 1))
                    act.activation(rstd[:, :], va[:, :], ACT.Exp, scale=-0.5).then_inc(done, 1)

                def exps(j, q):
                    act.wait_ge(sub_done, gv(t, j, 4, q + 1))
                    e = strided(E[:, j.mod(2), 2 * q, 0, 0:1], [[HI, 2 * HEADS], [1, N]])
                    s = strided(S[:, 2 * q, 0, 0:1], [[N, 2 * HEADS], [1, N]])
                    act.activation(e, s, ACT.Exp).then_inc(exp_done, 1)

                def evac_k(j):
                    act.wait_ge(k_mm, gv(t, j, 1, 1))
                    act.activation(flat(KT), pA0[0:R, 0:TOK], ACT.Identity, bias=cols[:, t, BK:BK + 1]).then_inc(kT_done, 1)

                def hidden(j, k):
                    act.wait_ge(fc1_mm, gv(t, j, 3, k + 1))
                    act.activation(hT[:, k], (pD0, pD1, pD0)[k][:, 0:TOK], gelu, bias=b1c[:, t, k:k + 1])\
                       .then_inc(gelu_done, 1)

                def iteration(a, b, c, d):
                    for p in range(P):
                        if c:
                            evac_et(c, p)
                        if p in (2, 4, 6) and b:
                            exps(b, p // 2 - 1)
                        if p == 0:
                            if d:
                                evac_o(d)
                            if a:
                                square(a, ctr1_mm, pA0, sq1, sq1_done)
                        if p == 1 and a:
                            inverse_std(a, var1_mm, pA1, va1, rs1, va1_done, rs1_done)
                        if p == 2 and d:
                            square(d, ctr2_mm, pD1, sq2, sq2_done)
                        if p == 3 and d:
                            inverse_std(d, var2_mm, pD0, va2, rs2, va2_done, rs2_done)
                        if p == 5 and a:
                            evac_k(a)
                        if p == 6 and d:
                            hidden(d, 0)
                            hidden(d, 1)
                        if p == 7:
                            if d:
                                hidden(d, 2)
                            if b:
                                exps(b, 3)

                sweep(act, t, iteration)

            def store_tm(j):
                b = j.mod(4)
                act.wait_ge(to_done, j.val(1, 1))
                act.dma_start(of_step(o_tm, j), tm[:, b])\
                   .then_inc(to_out[b], 16)

            for c in range(UN):
                store_tm(Step(0, c))
            with act.Fori(1, STEPS // UN) as u:
                for c in range(UN):
                    store_tm(Step(u, c))
            for b in range(4):
                act.wait_ge(to_out[b], 16 * STEPS // 4)

        @block.vector
        def _(dve):
            chained = [0]

            def chain(ins):
                chained[0] += 1
                ins.then_inc(fold, 1)
                dve.wait_ge(fold, chained[0])

            dve.wait_ge(zeroed, len(CLEARED) + 1)
            dve.wait_ge(const_in, 16 * len(consts))
            for t, ph in enumerate(PH):
                for r in (0, HI):
                    chain(dve.tensor_scalar(neg[r:r + N, t], regions[r:r + N], ph["neg"], None, ALU.mult))
            tables = 0
            for k, (_, ts_) in enumerate(TABLES):
                dve.wait_ge(idx_in, 16 * (k + 1))
                chain(dve.tensor_copy(idx_f[:, :], idx_i[:, :]))
                if k:
                    dve.wait_ge(tab_mm, 1)
                dve.tensor_scalar(oh_lo[:, :], idx_f[:, :], kcol[:, 0:1], None, ALU.is_equal)
                dve.tensor_scalar(oh_hi[:, :], idx_f[:, :], kcol[:, 1:2], None, ALU.is_equal).then_inc(onehot, 1)
                for t in ts_:
                    tables += 1
                    dve.wait_ge(tab_mm, tables)
                    for r in (0, HI):
                        src = strided(bank[2 + t][r:r + N, 0:1], [[1, HEADS], [HEADS, N]])
                        chain(dve.tensor_copy(bias[r:r + N, t, 0].rearrange("p (h m) -> p h m", m=N), src))
                        for kind in range(1, 4):
                            if PH[t]["shift"]:
                                dve.tensor_tensor(
                                    bias[r:r + N, t, kind].rearrange("p (h m) -> p h m", m=N),
                                    bias[r:r + N, t, 0].rearrange("p (h m) -> p h m", m=N),
                                    strided(neg[r:r + N, t, kind - 1, 0:1], [[0, HEADS], [1, N]]), ALU.add)
            dve.wait_ge(bias_mm, NPH)
            QS = float(D) ** -0.5
            for t in range(NPH):
                m = bank[6]
                o = 8 * t
                chain(dve.tensor_tensor(cols[:, t, BQ:BV + 1], cols[:, t, BQ:BV + 1], m[0:R, o:o + 3], ALU.add))
                chain(dve.tensor_scalar(cols[:, t, BQ:BQ + 1], cols[:, t, BQ:BQ + 1], QS, None, ALU.mult))
                chain(dve.tensor_tensor(b1c[:, t], b1c[:, t], m[:, o + 3:o + 6], ALU.add))
                ga = cols[:, t, GA1:GA1 + 1]
                dve.tensor_scalar(wq[:, t], wq[:, t], ga, QS, ALU.mult, ALU.mult)
                dve.tensor_scalar(wk[:, t], wk[:, t], ga, None, ALU.mult)
                dve.tensor_scalar(wv[:, t].rearrange("p (i c) -> p i c", i=2),
                                  strided(wvr[:, t, 0:1], [[HI, 2], [1, C]]), ga, None, ALU.mult)
                chain(dve.tensor_scalar(w1[:, t], w1[:, t], cols[:, t, GA2:GA2 + 1], None, ALU.mult))
            n_fold = chained[0]

            def spread_x(j):
                b = j.mod(4)
                dve.wait_ge(tm_in[b], 16 * j.uses(4) + 16)
                if not (isinstance(j.u, int) and j.u == 0):
                    dve.wait_ge(tr_done, j.val(1, -3))
                src = strided(tm[:, b, 0, 0:1], [[C, TK], [TK * C, 2], [1, C]])
                dst = strided(tz[:, b, 0, 0:1], [[128, TK], [HI, 2], [1, C]])
                dve.tensor_copy(dst, src).then_inc(tz_done, 1)

            for c in range(UN):
                spread_x(Step(0, c))
            with dve.Fori(1, STEPS // UN) as u:
                for c in range(UN):
                    spread_x(Step(u, c))
            for b in range(4):
                dve.wait_ge(cm_out[b], 16 * STEPS // 4)

            for t in range(NPH):
                s = PH[t]["shift"]

                def scores(j, p):
                    dve.wait_ge(s_mm, gv(t, j, P, p + 1))
                    if s:
                        last = (j.val(1, 0) % G + 1) // G
                        kind = 2 * last + (1 if p == P - 1 else 0)
                        bi = strided(bias[:, t, bass.ds(kind, 1), 0:1], [[1, HN]])
                    else:
                        bi = bias[:, t, 0]
                    if p % 2 == 0 and not (isinstance(j.u, int) and j.c == 0 and t == 0):
                        dve.wait_ge(exp_done, gv(t, j, 4, p // 2 - 3))
                    dve.tensor_tensor(strided(S[:, p, 0, 0:1], [[1, HN]]), pS[0:M2, 0:HN], bi, ALU.add)\
                       .then_inc(s_done, 1)

                def maxima(j, q):
                    dve.wait_ge(s_done, gv(t, j, P, 2 * q + 2))
                    g = strided(S[:, 2 * q, 0, 0:1], [[N, 2 * HEADS], [1, N]])
                    m = mx[:, 2 * HEADS * q:2 * HEADS * (q + 1)]
                    dve.tensor_reduce(m, g, AX.X, ALU.max).then_inc(mx_done, 1)
                    dve.wait_ge(mx_done, gv(t, j, 4, q + 1))
                    mb = strided(mx[:, 2 * HEADS * q:2 * HEADS * q + 1], [[1, 2 * HEADS], [0, N]])
                    dve.tensor_tensor(g, g, mb, ALU.subtract).then_inc(sub_done, 1)

                def sums(j, q):
                    b = j.mod(2)
                    dve.wait_ge(exp_done, gv(t, j, 4, q + 1))
                    e = strided(E[:, b, 2 * q, 0, 0:1], [[HI, 2 * HEADS], [1, N]])
                    h = slice(2 * HEADS * q, 2 * HEADS * (q + 1))
                    dve.tensor_reduce(sm[:, h], e, AX.X, ALU.add).then_inc(sum_done, 1)
                    dve.wait_ge(sum_done, gv(t, j, 4, q + 1))
                    dve.reciprocal(rs[:, b, h], sm[:, h]).then_inc(rcp_done, 1)

                def normal1(j):
                    dve.wait_ge(rs1_done, gv(t, j, 1, 1))

                    def windows(p0, n, j0, c0, w):
                        src = [[WIN, n], [W, WIN], [1, w]]
                        return dve.tensor_tensor(
                            strided(xn1[:, p0, 0, j0:j0 + 1], [[N, n], [WIN, WIN], [1, w]]),
                            strided(pA0[0:R, c0:c0 + 1], src), strided(rs1[:, c0:c0 + 1], src), ALU.mult)

                    if s:
                        windows(0, P - 1, 0, s, WIN)
                        windows(P - 1, 1, 0, W - WIN + s, WIN - s)
                        ins = windows(P - 1, 1, WIN - s, 0, s)
                    else:
                        ins = windows(0, P, 0, 0, WIN)
                    ins.then_inc(xn1_done, 1)

                def evac_q(j):
                    dve.wait_ge(q_mm, gv(t, j, 1, 1))
                    for r in (0, HI):
                        src = pA1[r:r + C, 0:TOK].rearrange("p (a n) -> p a n", n=N)
                        ins = dve.tensor_scalar(Qbd[r:r + C, j.mod(2), :, r:r + N], src, cols[r:r + C, t, BQ:BQ + 1], None, ALU.add)
                    ins.then_inc(q_done, 1)

                def evac_v(j, half):
                    dve.wait_ge(v_mm, gv(t, j, 2, half + 1))
                    src_bank = (pA1, pA0)[half]
                    for odd in range(2):
                        src = strided(src_bank[0:N, odd * D:odd * D + 1], [[C, P], [2 * D, HP], [1, D]])
                        dst = strided(V2[HI * odd:HI * odd + N, j.mod(4), half * P, odd * D:odd * D + 1],
                                      [[VC, P], [C + 2 * D, HP], [1, D]])
                        ins = dve.tensor_copy(dst, src)
                    ins.then_inc(v_done, 1)

                def residual1(j):
                    dve.wait_ge(proj_mm, gv(t, j, 1, 1))
                    if not (isinstance(j.u, int) and j.c == 0 and t == 0):
                        dve.wait_ge(x2_done, gv(t, j, 1, 0))
                    y = pD0[0:R, 0:TOK].rearrange("p (r c) -> p r c", r=WIN)
                    x = xin[:, j.mod(4)].rearrange("p (r c) -> p r c", r=WIN)
                    bp = cols[:, t, BP:BP + 1]
                    ins = dve.scalar_tensor_tensor(x1[:, :, s:W], y[:, :, 0:W - s], bp, x[:, :, s:W], ALU.add, ALU.add)
                    if s:
                        ins = dve.scalar_tensor_tensor(x1[:, :, 0:s], y[:, :, W - s:W], bp, x[:, :, 0:s],
                                                       ALU.add, ALU.add)
                    ins.then_inc(x1_done, 1)

                def normal2(j):
                    dve.wait_ge(rs2_done, gv(t, j, 1, 1))
                    dve.tensor_tensor(xn2[:, :], pD1[0:R, 0:TOK], rs2[:, :], ALU.mult).then_inc(xn2_done, 1)

                def residual2(j):
                    b = j.mod(2)
                    dve.wait_ge(fc2_mm, gv(t, j, 1, 1))
                    if not (isinstance(j.u, int) and j.c < 2):
                        dve.wait_ge(out_st[b], j.uses(2) * 32 + t * 32 * STEPS // 2)
                    dve.wait_ge(x1_done, gv(t, j, 1, 1))
                    dve.scalar_tensor_tensor(xout[:, b], pD1[0:R, 0:TOK], cols[:, t, B2:B2 + 1],
                                             x1[:, :, :].rearrange("p r c -> p (r c)"), ALU.add, ALU.add)\
                       .then_inc(x2_done, 1)

                def iteration(a, b, c, d):
                    for p in range(P):
                        if b:
                            scores(b, p)
                            if p % 2:
                                maxima(b, p // 2)
                        if p == 0 and c:
                            sums(c, 3)
                        if p in (2, 4, 6) and b:
                            sums(b, p // 2 - 1)
                        if p == 2 and d:
                            residual1(d)
                        if p == 3 and a:
                            normal1(a)
                        if p == 4 and d:
                            normal2(d)
                        if p == 5 and a:
                            evac_q(a)
                        if p == 6 and a:
                            evac_v(a, 0)
                        if p == 7:
                            if a:
                                evac_v(a, 1)
                            if d:
                                residual2(d)

                sweep(dve, t, iteration)

            def gather_tm(j):
                b = j.mod(4)
                dve.wait_ge(tr2_done, j.val(1, 1))
                if not (isinstance(j.u, int) and j.u == 0):
                    dve.wait_ge(to_out[b], 16 * j.uses(4))
                src = strided(bank[j.mod(2)][0:TP, 0:1], [[R, TK], [HI, 2], [1, C]])
                dst = strided(tm[:, b, 0, 0:1], [[C, TK], [TK * C, 2], [1, C]])
                dve.tensor_copy(dst, src).then_inc(to_done, 1)

            for c in range(UN):
                gather_tm(Step(0, c))
            with dve.Fori(1, STEPS // UN) as u:
                for c in range(UN):
                    gather_tm(Step(u, c))

        @block.tensor
        def _(pe):
            mm = pe.matmul
            pe.wait_ge(const_in, 16 * len(consts))
            pe.wait_ge(par_in, 16 * len(par))
            for k, (_, ts_) in enumerate(TABLES):
                pe.wait_ge(onehot, k + 1)
                for t in ts_:
                    for r in (0, HI):
                        for m in range(N):
                            o = bank[2 + t][r:r + N, HEADS * m:HEADS * (m + 1)]
                            mm(o, strided(oh_lo[:, m:m + 1], [[N, N]]), tab[:, t, 0], start=True, stop=False)
                            last = mm(o, strided(oh_hi[:, m:m + 1], [[N, N]]), tab[:, t, 1], start=False, stop=True)
                    last.then_inc(tab_mm, 1)
            for t in range(NPH):
                o = 8 * t
                be1, be2 = cols[:, t, BE1:BE1 + 1], cols[:, t, BE2:BE2 + 1]
                for i, w in enumerate((wq, wk, wvr)):
                    mm(bank[6][0:R, o + i:o + i + 1], w[:, t], be1, start=True, stop=True)
                for k in range(3):
                    last = mm(bank[6][:, o + 3 + k:o + 4 + k], w1[:, t, k], be2, start=True, stop=True)
                last.then_inc(bias_mm, 1)

            def transpose_x(j):
                b = j.mod(4)
                pe.wait_ge(tz_done, j.val(1, 1))
                if not (isinstance(j.u, int) and j.c < 2 and j.u == 0):
                    pe.wait_ge(cm_done, j.val(1, -1))
                for k in range(TK):
                    last = pe.transpose(bank[j.mod(2)][0:R, k * TP:(k + 1) * TP], tz[:, b, k, 0:R], ident[0:TP, 0:TP])
                last.then_inc(tr_done, 1)

            for c in range(UN):
                transpose_x(Step(0, c))
            with pe.Fori(1, STEPS // UN) as u:
                for c in range(UN):
                    transpose_x(Step(u, c))
            pe.wait_ge(cm_done, STEPS)

            for t in range(NPH):
                s = PH[t]["shift"]

                def first(j):
                    return isinstance(j.u, int) and j.c == 0

                def transposes(j, p):
                    if p % 2 == 0:
                        pe.wait_ge(norm_done, gv(t, j, 4, p // 2 + 1))
                    if not (first(j) and t == 0 and p == 0):
                        pe.wait_ge(et_done, gv(t, j, P, p))
                    for k in range(HP):
                        last = pe.transpose(pT[0:M2, k * M2:(k + 1) * M2],
                                            strided(E[:, j.mod(2), p, 2 * k, 0:1], [[1, M2]]), ident[0:M2, 0:M2])
                    last.then_inc(tr_mm, 1)

                def scores(j, p):
                    if p == 0:
                        pe.wait_ge(q_done, gv(t, j, 1, 1))
                    if p % (P // 2) == 0:
                        pe.wait_ge(kbd_done, gv(t, j, 2, 1 + 2 * p // P))
                    if not (first(j) and t == 0 and p == 0):
                        pe.wait_ge(s_done, gv(t, j, P, p))
                    mm(pS[0:M2, 0:HN], Qbd[:, j.mod(2), p, 0:M2],
                       strided(Kbd[:, j.mod(2), p, 0, 0:1], [[1, HN]]), start=True, stop=True).then_inc(s_mm, 1)

                def values(j, p):
                    pe.wait_ge(et_done, gv(t, j, P, p + 1))
                    if p == 0:
                        pe.wait_ge(v_done, gv(t, j, 2, 2))
                        if not (first(j) and t == 0):
                            pe.wait_ge(oT_done, gv(t, j, 1, 0))
                    for w in range(2):
                        for k in range(HP):
                            last = mm(pO[w][0:C, N * p:N * (p + 1)],
                                      V2[:, j.mod(4), 2 * p + w, C * k:C * (k + 1)],
                                      ET[:, p % 2, k, HI * w:HI * w + N], start=(k == 0), stop=(k == HP - 1))
                    last.then_inc(pv_mm, 1)

                def center1(j):
                    pe.wait_ge(xin_in[j.mod(4)], j.uses(4) * 32 + 32 + t * 32 * STEPS // 4)
                    if not (first(j) and t == 0):
                        pe.wait_ge(v_done, gv(t, j, 2, 0))
                    mm(pA0[0:R, 0:TOK], center[:, :], xin[:, j.mod(4)], start=True, stop=True).then_inc(ctr1_mm, 1)

                def var1(j):
                    pe.wait_ge(sq1_done, gv(t, j, 1, 1))
                    mm(pA1[0:R, 0:TOK], mean[:, :], sq1[:, :], start=True, stop=True).then_inc(var1_mm, 1)

                def query_key(j):
                    pe.wait_ge(xn1_done, gv(t, j, 1, 1))
                    pe.wait_ge(va1_done, gv(t, j, 1, 1))
                    mm(pA1[0:R, 0:TOK], wq[:, t], flat(xn1), start=True, stop=True).then_inc(q_mm, 1)
                    mm(pA0[0:R, 0:TOK], wk[:, t], flat(xn1), start=True, stop=True).then_inc(k_mm, 1)

                def value(j, half):
                    pe.wait_ge((q_done, kT_done)[half], gv(t, j, 1, 1))
                    for i in range(P // 2):
                        x = strided(xn1[:, half * P // 2 + i, 0, 0:1], [[1, N]])
                        last = mm((pA1, pA0)[half][0:N, 2 * C * i:2 * C * (i + 1)], x,
                                  wv[:, t], start=True, stop=True)
                    last.then_inc(v_mm, 1)

                def project(j):
                    pe.wait_ge(oT_done, gv(t, j, 1, 1))
                    rolled = strided(oT[:, 0, 0:1], [[WIN, WIN], [N, P], [1, WIN]])
                    mm(pD0[0:R, 0:TOK], wp[:, t], rolled, start=True, stop=True).then_inc(proj_mm, 1)

                def center2(j):
                    pe.wait_ge(x1_done, gv(t, j, 1, 1))
                    if not (first(j) and t == 0):
                        pe.wait_ge(x2_done, gv(t, j, 1, 0))
                    mm(pD1[0:R, 0:TOK], center[:, :], x1[:, :, :].rearrange("p r c -> p (r c)"),
                       start=True, stop=True).then_inc(ctr2_mm, 1)

                def var2(j):
                    pe.wait_ge(sq2_done, gv(t, j, 1, 1))
                    mm(pD0[0:R, 0:TOK], mean[:, :], sq2[:, :], start=True, stop=True).then_inc(var2_mm, 1)

                def up(j, k):
                    if k == 0:
                        pe.wait_ge(xn2_done, gv(t, j, 1, 1))
                    if k == 2:
                        pe.wait_ge(gelu_done, gv(t, j, 3, 1))
                    mm((pD0, pD1, pD0)[k][:, 0:TOK], w1[:, t, k], xn2[:, :], start=True, stop=True).then_inc(fc1_mm, 1)

                def down(j):
                    for k in range(3):
                        if k:
                            pe.wait_ge(gelu_done, gv(t, j, 3, k + 1))
                        last = mm(pD1[0:R, 0:TOK], w2[:, t, k], hT[:, k], start=(k == 0), stop=(k == 2))
                    last.then_inc(fc2_mm, 1)

                def iteration(a, b, c, d):
                    for p in range(P):
                        if c:
                            transposes(c, p)
                        if b:
                            scores(b, p)
                        if p == 0 and a:
                            center1(a)
                        if p == 1:
                            if a:
                                var1(a)
                            if d:
                                project(d)
                        if p == 2 and d:
                            center2(d)
                        if p == 3 and d:
                            var2(d)
                        if p == 4 and a:
                            query_key(a)
                        if p == 5:
                            if a:
                                value(a, 0)
                            if d:
                                up(d, 0)
                                up(d, 1)
                        if p == 6:
                            if a:
                                value(a, 1)
                            if d:
                                up(d, 2)
                        if p == 7 and d:
                            pe.wait_ge(gelu_done, gv(t, d, 3, 2))
                            down(d)
                        if c:
                            values(c, p)

                sweep(pe, t, iteration)

            pe.wait_ge(x2_done, NPH * STEPS)

            def transpose_out(j):
                b = j.mod(4)
                pe.wait_ge(cm_in[b], 16 * j.uses(4) + 16)
                if not (isinstance(j.u, int) and j.c < 2 and j.u == 0):
                    pe.wait_ge(to_done, j.val(1, -1))
                for k in range(TK):
                    last = pe.transpose(bank[j.mod(2)][0:TP, k * R:(k + 1) * R],
                                        strided(cm[:, b, k:k + 1], [[TK, TP]]), ident[0:R, 0:R])
                last.then_inc(tr2_done, 1)

            for c in range(UN):
                transpose_out(Step(0, c))
            with pe.Fori(1, STEPS // UN) as u:
                for c in range(UN):
                    transpose_out(Step(u, c))


def constants():
    eye = np.eye(128, dtype=np.float32)
    center = np.zeros((R, R), np.float32)
    mean = np.zeros((R, R), np.float32)
    headmask = np.zeros((R, HEADS), np.float32)
    for r in (0, HI):
        mean[r:r + C, r:r + C] = 1.0 / C
        center[r:r + C, r:r + C] = np.eye(C) - 1.0 / C
        for h in range(HEADS):
            headmask[r + D * h:r + D * (h + 1), h] = 1.0
    kcol = np.stack([np.arange(128), np.arange(128) + 128], 1).astype(np.float32)
    i, j = np.divmod(np.arange(N), WIN)
    col = (j[:, None] < WIN - SHIFT) != (j[None, :] < WIN - SHIFT)
    row = (i[:, None] < WIN - SHIFT) != (i[None, :] < WIN - SHIFT)
    regions = np.stack([col, row, col | row], 1).astype(np.float32)
    rel = ((i[:, None] - i[None, :] + WIN - 1) * (2 * WIN - 1) + j[:, None] - j[None, :] + WIN - 1)
    return dict(ident=eye, center=center, mean=mean, headmask=headmask, kcol=kcol, regions=regions,
                rel_const=rel.reshape(-1).astype(np.int32))


def kernel(**inputs):
    import concourse.bacc as bacc
    from concourse.bass_utils import run_bass_kernel_spmd

    nc = bacc.Bacc("TRN2", target_bir_lowering=False, num_devices=1)
    arrays, aps = {}, {}
    for name, a in {**inputs, **constants()}.items():
        a = np.ascontiguousarray(a)
        arrays[f"in_{name}"] = a
        aps[name] = nc.dram_tensor(f"in_{name}", a.shape, mybir.dt.from_np(a.dtype), kind="ExternalInput").ap()
    out = nc.dram_tensor("out", (B, H, W, C), mybir.dt.float32, kind="ExternalOutput").ap()
    build(nc, aps, out)
    r = run_bass_kernel_spmd(nc, [arrays], core_ids=[0])
    return r.results[0]["out"]
```

```python
from contextlib import ExitStack

import numpy as np

import concourse.bass as bass
from concourse import mybir

B, H, W, C = 32, 56, 56, 48
HEADS, WIN, SHIFT = 6, 7, 3
D = C // HEADS
N = WIN * WIN
HID = 4 * C
REL = (2 * WIN - 1) ** 2
EPS = 1e-5

HI = 64
R = HI + C
M2 = HI + N
PAIRS = B // 2
G = H // WIN
STEPS = PAIRS * G
TOK = WIN * W
P = W // WIN
HN = HEADS * N
IMG = H * W
TP, TK = 98, 4
UN = 4
HP = HEADS // 2
VC = HP * C


class Step:

    def __init__(self, u, c):
        self.u, self.c = u, c

    def val(self, scale, add):
        return self.u * (UN * scale) + (self.c * scale + add)

    def uses(self, of):
        return self.u * (UN // of) + self.c // of

    def mod(self, of):
        return self.c % of


def build(nc, A, out):
    fp32, i32 = mybir.dt.float32, mybir.dt.int32
    ALU, ACT, AX = mybir.AluOpType, mybir.ActivationFunctionType, mybir.AxisListType
    ctx = ExitStack()
    with ctx:
        def sb(name, shape, dt=fp32):
            return ctx.enter_context(nc.sbuf_tensor(name, shape, dt))

        def sem(name):
            return ctx.enter_context(nc.semaphore(name))

        L0, L1 = "L0_conv_", "L1_conv_"
        mlp1 = dict(g1=L1 + "ln1_g", b1=L1 + "ln1_b", g2=L1 + "ln2_g", b2=L1 + "ln2_b",
                    w1=L1 + "mlp_w1", c1=L1 + "mlp_b1", w2=L1 + "mlp_w2", c2=L1 + "mlp_b2",
                    gelu=ACT.Gelu_apprx_tanh, index=L1 + "rel_index")
        PH = [
            dict(g1=L0 + "norm1_w", b1=L0 + "norm1_b", g2=L0 + "norm2_w", b2=L0 + "norm2_b",
                 w1=L0 + "fc1_w", c1=L0 + "fc1_b", w2=L0 + "fc2_w", c2=L0 + "fc2_b",
                 wqkv=L0 + "qkv_w", bqkv=L0 + "qkv_b", wp=L0 + "proj_w", bp=L0 + "proj_b",
                 table=L0 + "rpb_table", index="rel_const", gelu=ACT.Gelu, shift=SHIFT, neg=-100.0),
            dict(mlp1, wqkv=L1 + "w_qkv_w", bqkv=L1 + "w_qkv_b", wp=L1 + "w_proj_w",
                 bp=L1 + "w_proj_b", table=L1 + "w_rel", shift=0, neg=0.0),
            dict(mlp1, wqkv=L1 + "s_qkv_w", bqkv=L1 + "s_qkv_b", wp=L1 + "s_proj_w",
                 bp=L1 + "s_proj_b", table=L1 + "s_rel", shift=SHIFT, neg=-1e9),
        ]
        NPH = len(PH)

        scratch = [nc.dram_tensor(f"xT{k}", (PAIRS, R, IMG), fp32, kind="Internal").ap()
                   for k in range(NPH + 1)]
        x_tm = A["x"].rearrange("(P i) h w c -> P i (h w c)", i=2)\
                     .rearrange("P i (g p e) -> P g p i e", g=G, p=TP)
        o_tm = out.rearrange("(P i) h w c -> P i (h w c)", i=2)\
                  .rearrange("P i (g p e) -> P g p i e", g=G, p=TP)

        ident = sb("ident", [128, 128])
        center = sb("center", [R, R])
        mean = sb("mean", [R, R])
        headmask = sb("headmask", [R, HEADS])
        eps = sb("eps", [R, 1])
        kcol = sb("kcol", [128, 2])
        regions = sb("regions", [M2, 3, N])
        wq = sb("wq", [R, NPH, R])
        wk = sb("wk", [R, NPH, R])
        wvr = sb("wvr", [R, NPH, R])
        wv = sb("wv", [R, NPH, 2 * C])
        wp = sb("wp", [R, NPH, R])
        w1 = sb("w1", [R, NPH, 3, 128])
        w2 = sb("w2", [128, NPH, 3, R])
        GA1, BE1, GA2, BE2, BQ, BK, BV, BP, B2 = range(9)
        cols = sb("cols", [R, NPH, 9])
        b1c = sb("b1c", [128, NPH, 3])
        bias = sb("bias", [M2, NPH, 4, HN])

        Qbd = sb("Qbd", [R, 2, P, 128])
        V2 = sb("V2", [M2, 4, 2 * P, VC])
        E = sb("E", [M2, 2, P, HEADS, HI])
        oT = sb("oT", [R, P, N])

        with ExitStack() as early:
            def tmp(name, shape, dt=fp32):
                return early.enter_context(nc.sbuf_tensor(name, shape, dt))

            tm = tmp("tm", [TP, 4, 2, TK * C])
            tz = tmp("tz", [TP, 4, TK, 128])
            cm = tmp("cm", [R, 4, TOK])
            idx_i = tmp("idx_i", [128, N * N], i32)
            idx_f = tmp("idx_f", [128, N * N])
            oh_lo = tmp("oh_lo", [128, N * N])
            oh_hi = tmp("oh_hi", [128, N * N])
            tab = tmp("tab", [128, NPH, 2, HEADS])
            neg = tmp("neg", [M2, NPH, 3, N])

        xin = sb("xin", [R, 4, TOK])
        sq1 = sb("sq1", [R, TOK])
        va1 = sb("va1", [R, TOK])
        rs1 = sb("rs1", [R, TOK])
        xn1 = sb("xn1", [R, P, WIN, WIN])
        KT = sb("KT", [R, P, N])
        Kbd = sb("Kbd", [R, 2, P, HEADS, N])
        S = sb("S", [M2, P, HEADS, N])
        mx = sb("mx", [M2, P * HEADS])
        sm = sb("sm", [M2, P * HEADS])
        rs = sb("rs", [M2, 2, P * HEADS])
        ET = sb("ET", [M2, 2, HP, M2])
        x1 = sb("x1", [R, 2, WIN, W])
        sq2 = sb("sq2", [R, TOK])
        va2 = sb("va2", [R, TOK])
        rs2 = sb("rs2", [R, TOK])
        xn2 = sb("xn2", [R, TOK])
        hT = sb("hT", [128, 3, TOK])
        xout = sb("xout", [R, 2, TOK])

        bank = [ctx.enter_context(nc.psum_tensor(f"bank{k}", [128, 512], fp32)) for k in range(8)]
        pS, pT, pO0, pO1, pA0, pA1, pD0, pD1 = bank
        pO = [pO0, pO1]

        def strided(ap, dims):
            return bass.AP(ap.tensor, ap.offset, [list(ap.ap[0])] + [list(d) for d in dims])

        zeroed = sem("zeroed")
        const_in = sem("const_in")
        par_in = sem("par_in")
        idx_in = sem("idx_in")
        onehot = sem("onehot")
        tab_mm = sem("tab_mm")
        tab_done = sem("tab_done")
        bias_mm = sem("bias_mm")
        fold = sem("fold")
        tm_in = [sem(f"tm_in{b}") for b in range(4)]
        tz_done, tr_done, cm_done = sem("tz_done"), sem("tr_done"), sem("cm_done")
        cm_out = [sem(f"cm_out{b}") for b in range(4)]
        cm_in = [sem(f"cm_in{b}") for b in range(4)]
        tr2_done, to_done = sem("tr2_done"), sem("to_done")
        to_out = [sem(f"to_out{b}") for b in range(4)]
        xin_in = [sem(f"xin_in{b}") for b in range(4)]
        out_st = [sem(f"out_st{b}") for b in range(2)]
        ctr1_mm, sq1_done, var1_mm, va1_done, rs1_done, xn1_done = (
            sem(n) for n in ("ctr1_mm", "sq1_done", "var1_mm", "va1_done", "rs1_done", "xn1_done"))
        q_mm, k_mm, v_mm = sem("q_mm"), sem("k_mm"), sem("v_mm")
        q_done, kT_done = sem("q_done"), sem("kT_done")
        kbd_done, v_done = sem("kbd_done"), sem("v_done")
        s_mm, s_done = sem("s_mm"), sem("s_done")
        mx_done, sub_done, exp_done, sum_done, rcp_done, norm_done = (
            sem(n) for n in ("mx_done", "sub_done", "exp_done", "sum_done", "rcp_done", "norm_done"))
        tr_mm, et_done = sem("tr_mm"), sem("et_done")
        pv_mm, oT_done = sem("pv_mm"), sem("oT_done")
        proj_mm, x1_done, ctr2_mm, sq2_done, var2_mm, va2_done, rs2_done, xn2_done = (
            sem(n) for n in ("proj_mm", "x1_done", "ctr2_mm", "sq2_done", "var2_mm", "va2_done",
                             "rs2_done", "xn2_done"))
        fc1_mm, gelu_done = sem("fc1_mm"), sem("gelu_done")
        fc2_mm, x2_done = sem("fc2_mm"), sem("x2_done")

        def col(t, j, v, o=0):
            return [(cols[r:r + C, t, j:j + 1], v[o:o + C].rearrange("(c a) -> c a", a=1)) for r in (0, HI)]

        def diag(tile, t, src):
            return [(tile[r:r + C, t, r:r + C], src) for r in (0, HI)]

        par = []
        for t, ph in enumerate(PH):
            wqkv, bqkv = A[ph["wqkv"]], A[ph["bqkv"]]
            for k, tile in enumerate((wq, wk, wvr)):
                par += diag(tile, t, wqkv[:, k * C:(k + 1) * C])
            par += diag(wp, t, A[ph["wp"]])
            for j, v, o in ((GA1, ph["g1"], 0), (BE1, ph["b1"], 0), (GA2, ph["g2"], 0), (BE2, ph["b2"], 0),
                            (BQ, ph["bqkv"], 0), (BK, ph["bqkv"], C), (BV, ph["bqkv"], 2 * C),
                            (BP, ph["bp"], 0), (B2, ph["c2"], 0)):
                par += col(t, j, A[v], o)
            for k, lo, r, h0, n in ((0, 0, 0, 0, 128), (1, 0, 0, 128, 64), (1, 64, HI, 0, 64), (2, 0, HI, 64, 128)):
                par.append((w1[r:r + C, t, k, lo:lo + n], A[ph["w1"]][:, h0:h0 + n]))
                par.append((w2[lo:lo + n, t, k, r:r + C], A[ph["w2"]][h0:h0 + n, :]))
                par.append((b1c[lo:lo + n, t, k:k + 1], A[ph["c1"]][h0:h0 + n].rearrange("(c a) -> c a", a=1)))
            par.append((tab[:, t, 0, :], A[ph["table"]][0:128, :]))
            par.append((tab[0:REL - 128, t, 1, :], A[ph["table"]][128:REL, :]))
        consts = [(ident[:, :], A["ident"]), (center[:, :], A["center"]), (mean[:, :], A["mean"]),
                  (headmask[:, :], A["headmask"]), (kcol[:, :], A["kcol"]),
                  (regions[0:N, :, :], A["regions"]), (regions[HI:M2, :, :], A["regions"])]
        TABLES = [("rel_const", [0]), (L1 + "rel_index", [1, 2])]
        CLEARED = [wq, wk, wvr, wp, w1, w2, cols, b1c, bias, Qbd, V2, E, oT, tz, tab, neg]

        def flat(tile):
            ap = tile[:]
            n = 1
            for d in ap.shape[1:]:
                n *= d
            return strided(ap, [[1, n]])

        block = ctx.enter_context(nc.Block())

        def sweep(eng, t, iteration):
            ahead = (1, 0, -1, -2, -3)

            def peeled(i):
                iteration(*(Step(0, i + k) if 0 <= i + k < STEPS else None for k in ahead))

            for i in range(-1, 3):
                peeled(i)
            full = (STEPS - 5) // UN
            with eng.Fori(0, full) as u:
                for k in range(UN):
                    iteration(*(Step(u, 3 + k + o) for o in ahead))
            for i in range(3 + UN * full, STEPS + 3):
                peeled(i)

        SPLIT = WIN - SHIFT

        def piece(t, k, j, part):
            s = PH[t]["shift"]
            pair, g = j.val(1, 0) // G, j.val(1, 0) % G
            if part == 0:
                return scratch[k][bass.ds(pair, 1), :, bass.ds(g * TOK + s * W, SPLIT * W)]\
                    .rearrange("a r n -> (a r) n")
            if s:
                g, at = (j.val(1, 1)) % G, 0
            else:
                at = SPLIT * W
            return scratch[k][bass.ds(pair, 1), :, bass.ds(g * TOK + at, SHIFT * W)]\
                .rearrange("a r n -> (a r) n")

        def of_step(dram, j):
            pair, g = j.val(1, 0) // G, j.val(1, 0) % G
            return dram[bass.ds(pair, 1), bass.ds(g, 1)].rearrange("a b p i e -> (a b p) i e")

        def mine(part):
            return slice(0, SPLIT * W) if part == 0 else slice(SPLIT * W, TOK)

        def global_val(t, j, scale=1, add=0):
            return j.val(scale, add + t * STEPS * scale)

        gv = global_val

        @block.sync
        def _(sp):
            for to, of in consts:
                sp.dma_start(to, of).then_inc(const_in, 16)

            def load_x(j):
                b = j.mod(4)
                if not (isinstance(j.u, int) and j.u == 0):
                    sp.wait_ge(tz_done, j.val(1, -3))
                sp.dma_start(tm[:, b], of_step(x_tm, j))\
                  .then_inc(tm_in[b], 16)

            for c in range(UN):
                load_x(Step(0, c))
            for k, (index, _) in enumerate(TABLES):
                if k:
                    sp.wait_ge(onehot, 1)
                sp.dma_start(idx_i[:, :], A[index].rearrange("(a n) -> a n", a=1).to_broadcast([128, N * N])
                             if len(A[index].shape) == 1 else
                             A[index].rearrange("(a n) m -> a (n m)", a=1).to_broadcast([128, N * N]))\
                  .then_inc(idx_in, 16)
            with sp.Fori(1, STEPS // UN) as u:
                for c in range(UN):
                    load_x(Step(u, c))
            for b in range(4):
                sp.wait_ge(cm_out[b], 16 * STEPS // 4)

            for t in range(NPH):
                if t:
                    for b in range(2):
                        sp.wait_ge(out_st[b], 32 * t * STEPS // 2)

                def load(j):
                    b = j.mod(4)
                    if not (isinstance(j.u, int) and j.c < 4):
                        sp.wait_ge(x1_done, gv(t, j, 1, -3))
                    for part in range(2):
                        sp.dma_start(xin[:, b, mine(part)], piece(t, t, j, part)).then_inc(xin_in[b], 16)

                def store(j):
                    b = j.mod(2)
                    sp.wait_ge(x2_done, gv(t, j, 1, 1))
                    for part in range(2):
                        sp.dma_start(piece(t, t + 1, j, part), xout[:, b, mine(part)]).then_inc(out_st[b], 16)

                load(Step(0, 0))

                def iteration(a, b, c, d, e):
                    nxt = Step(a.u, a.c + 1) if a else None
                    if nxt and (not isinstance(nxt.u, int) or nxt.c < STEPS):
                        load(nxt)
                    if e:
                        store(e)

                sweep(sp, t, iteration)

            for b in range(2):
                sp.wait_ge(out_st[b], 32 * NPH * STEPS // 2)

            def load_cm(j):
                b = j.mod(4)
                if not (isinstance(j.u, int) and j.u == 0):
                    sp.wait_ge(tr2_done, j.val(1, -3))
                sp.dma_start(cm[:, b], scratch[NPH][bass.ds(j.val(1, 0) // G, 1), :, bass.ds((j.val(1, 0) % G) * TOK, TOK)]
                             .rearrange("a r n -> (a r) n")).then_inc(cm_in[b], 16)

            for c in range(UN):
                load_cm(Step(0, c))
            with sp.Fori(1, STEPS // UN) as u:
                for c in range(UN):
                    load_cm(Step(u, c))

        @block.gpsimd
        def _(pool):
            for tile in CLEARED:
                pool.memset(flat(tile), 0.0).then_inc(zeroed, 1)
            pool.memset(eps[:, :], EPS).then_inc(zeroed, 1)

            for t in range(NPH):
                def norm(j, q):
                    b = j.mod(2)
                    pool.wait_ge(rcp_done, gv(t, j, 4, q + 1))
                    e = strided(E[:, b, 2 * q, 0, 0:1], [[HI, 2 * HEADS], [1, N]])
                    r = strided(rs[:, b, 2 * HEADS * q:2 * HEADS * q + 1], [[1, 2 * HEADS], [0, N]])
                    pool.tensor_tensor(e, e, r, ALU.mult).then_inc(norm_done, 1)

                def spread_k(j, half):
                    if half == 0:
                        pool.wait_ge(kT_done, gv(t, j, 1, 1))
                    p0 = half * P // 2
                    k = strided(KT[:, p0, 0:1], [[N, P // 2], [0, HEADS], [1, N]])
                    m = strided(headmask[:, 0:1], [[0, P // 2], [1, HEADS], [0, N]])
                    pool.tensor_tensor(Kbd[:, j.mod(2), p0:p0 + P // 2], k, m, ALU.mult).then_inc(kbd_done, 1)

                def iteration(a, b, c, d, e):
                    if c:
                        norm(c, 2)
                        norm(c, 3)
                    if b:
                        norm(b, 0)
                    if a:
                        spread_k(a, 0)
                    if b:
                        norm(b, 1)
                    if a:
                        spread_k(a, 1)

                if t == 0:
                    pool.wait_ge(const_in, 16 * len(consts))
                sweep(pool, t, iteration)

        @block.scalar
        def _(act):
            act.wait_ge(zeroed, len(CLEARED) + 1)
            for to, of in par:
                act.dma_start(to, of).then_inc(par_in, 16)

            def evac_cm(j):
                b = j.mod(4)
                act.wait_ge(tr_done, j.val(1, 1))
                if not (isinstance(j.u, int) and j.u == 0):
                    act.wait_ge(cm_out[b], j.uses(4) * 16)
                src = strided(bank[j.mod(2)][0:R, 0:1], [[1, TP], [TP, TK]])
                act.activation(strided(cm[:, b, 0:1], [[TK, TP], [1, TK]]), src, ACT.Copy).then_inc(cm_done, 1)
                act.wait_ge(cm_done, j.val(1, 1))
                act.dma_start(scratch[0][bass.ds(j.val(1, 0) // G, 1), :, bass.ds((j.val(1, 0) % G) * TOK, TOK)]
                              .rearrange("a r n -> (a r) n"), cm[:, b]).then_inc(cm_out[b], 16)

            for c in range(UN):
                evac_cm(Step(0, c))
            with act.Fori(1, STEPS // UN) as u:
                for c in range(UN):
                    evac_cm(Step(u, c))
            for b in range(4):
                act.wait_ge(cm_out[b], 16 * STEPS // 4)

            act.preload_act_table_set("natural_log_exp_and_others")
            for t in range(NPH):
                gelu = PH[t]["gelu"]

                def evac_et(j, p):
                    act.wait_ge(tr_mm, gv(t, j, P, p + 1))
                    act.activation(flat3(ET[:, p % 2]), pT[0:M2, 0:HP * M2], ACT.Copy).then_inc(et_done, 1)

                def flat3(ap):
                    return strided(ap, [[1, HP * M2]])

                def evac_o(j):
                    act.wait_ge(pv_mm, gv(t, j, P, P))
                    for w in range(2):
                        r = HI * w
                        ins = act.activation(strided(oT[r:r + C, 0, 0:1], [[1, TOK]]), pO[w][0:C, 0:TOK],
                                             ACT.Identity, bias=cols[r:r + C, t, BV:BV + 1])
                    ins.then_inc(oT_done, 1)

                def square(j, mm, src, dst, done):
                    act.wait_ge(mm, gv(t, j, 1, 1))
                    act.activation(dst[:, :], src[0:R, 0:TOK], ACT.Square).then_inc(done, 1)

                def inverse_std(j, mm, src, va, rstd, va_done, done):
                    act.wait_ge(mm, gv(t, j, 1, 1))
                    act.activation(va[:, :], src[0:R, 0:TOK], ACT.Ln, bias=eps[:, 0:1]).then_inc(va_done, 1)
                    act.wait_ge(va_done, gv(t, j, 1, 1))
                    act.activation(rstd[:, :], va[:, :], ACT.Exp, scale=-0.5).then_inc(done, 1)

                def exps(j, q):
                    act.wait_ge(sub_done, gv(t, j, 4, q + 1))
                    e = strided(E[:, j.mod(2), 2 * q, 0, 0:1], [[HI, 2 * HEADS], [1, N]])
                    s = strided(S[:, 2 * q, 0, 0:1], [[N, 2 * HEADS], [1, N]])
                    act.activation(e, s, ACT.Exp).then_inc(exp_done, 1)

                def evac_k(j):
                    act.wait_ge(k_mm, gv(t, j, 1, 1))
                    act.activation(flat(KT), pA0[0:R, 0:TOK], ACT.Identity, bias=cols[:, t, BK:BK + 1]).then_inc(kT_done, 1)

                def hidden(j, k):
                    act.wait_ge(fc1_mm, gv(t, j, 3, k + 1))
                    act.activation(hT[:, k], (pD0, pD1, pD0)[k][:, 0:TOK], gelu, bias=b1c[:, t, k:k + 1])\
                       .then_inc(gelu_done, 1)

                def iteration(a, b, c, d, e):
                    for p in range(P):
                        if p == 0 and d:
                            evac_o(d)
                        if c:
                            evac_et(c, p)
                        if p == 0:
                            if c:
                                exps(c, 3)
                            if e:
                                square(e, ctr2_mm, pD1, sq2, sq2_done)
                        if p == 1:
                            if a:
                                square(a, ctr1_mm, pA0, sq1, sq1_done)
                            if e:
                                inverse_std(e, var2_mm, pD0, va2, rs2, va2_done, rs2_done)
                        if p in (2, 6) and b:
                            exps(b, 0 if p == 2 else 2)
                        if p == 2 and a:
                            inverse_std(a, var1_mm, pA1, va1, rs1, va1_done, rs1_done)
                        if p == 3 and e:
                            hidden(e, 0)
                            hidden(e, 1)
                        if p == 4:
                            if e:
                                hidden(e, 2)
                                act.preload_act_table_set("natural_log_exp_and_others")
                            if b:
                                exps(b, 1)
                        if p == 5 and a:
                            evac_k(a)

                sweep(act, t, iteration)

            def store_tm(j):
                b = j.mod(4)
                act.wait_ge(to_done, j.val(1, 1))
                act.dma_start(of_step(o_tm, j), tm[:, b])\
                   .then_inc(to_out[b], 16)

            for c in range(UN):
                store_tm(Step(0, c))
            with act.Fori(1, STEPS // UN) as u:
                for c in range(UN):
                    store_tm(Step(u, c))
            for b in range(4):
                act.wait_ge(to_out[b], 16 * STEPS // 4)

        @block.vector
        def _(dve):
            chained = [0]

            def chain(ins):
                chained[0] += 1
                ins.then_inc(fold, 1)
                dve.wait_ge(fold, chained[0])

            dve.wait_ge(zeroed, len(CLEARED) + 1)
            dve.wait_ge(const_in, 16 * len(consts))
            for t, ph in enumerate(PH):
                for r in (0, HI):
                    chain(dve.tensor_scalar(neg[r:r + N, t], regions[r:r + N], ph["neg"], None, ALU.mult))
            tables = 0
            for k, (_, ts_) in enumerate(TABLES):
                dve.wait_ge(idx_in, 16 * (k + 1))
                chain(dve.tensor_copy(idx_f[:, :], idx_i[:, :]))
                if k:
                    dve.wait_ge(tab_mm, 1)
                dve.tensor_scalar(oh_lo[:, :], idx_f[:, :], kcol[:, 0:1], None, ALU.is_equal)
                dve.tensor_scalar(oh_hi[:, :], idx_f[:, :], kcol[:, 1:2], None, ALU.is_equal).then_inc(onehot, 1)
                for t in ts_:
                    tables += 1
                    dve.wait_ge(tab_mm, tables)
                    for r in (0, HI):
                        src = strided(bank[2 + t][r:r + N, 0:1], [[1, HEADS], [HEADS, N]])
                        chain(dve.tensor_copy(bias[r:r + N, t, 0].rearrange("p (h m) -> p h m", m=N), src))
                        for kind in range(1, 4):
                            if PH[t]["shift"]:
                                dve.tensor_tensor(
                                    bias[r:r + N, t, kind].rearrange("p (h m) -> p h m", m=N),
                                    bias[r:r + N, t, 0].rearrange("p (h m) -> p h m", m=N),
                                    strided(neg[r:r + N, t, kind - 1, 0:1], [[0, HEADS], [1, N]]), ALU.add)
            dve.wait_ge(bias_mm, NPH)
            QS = float(D) ** -0.5
            for t in range(NPH):
                m = bank[6]
                o = 8 * t
                chain(dve.tensor_tensor(cols[:, t, BQ:BV + 1], cols[:, t, BQ:BV + 1], m[0:R, o:o + 3], ALU.add))
                chain(dve.tensor_scalar(cols[:, t, BQ:BQ + 1], cols[:, t, BQ:BQ + 1], QS, None, ALU.mult))
                chain(dve.tensor_tensor(b1c[:, t], b1c[:, t], m[:, o + 3:o + 6], ALU.add))
                ga = cols[:, t, GA1:GA1 + 1]
                dve.tensor_scalar(wq[:, t], wq[:, t], ga, QS, ALU.mult, ALU.mult)
                dve.tensor_scalar(wk[:, t], wk[:, t], ga, None, ALU.mult)
                dve.tensor_scalar(wv[:, t].rearrange("p (i c) -> p i c", i=2),
                                  strided(wvr[:, t, 0:1], [[HI, 2], [1, C]]), ga, None, ALU.mult)
                chain(dve.tensor_scalar(w1[:, t], w1[:, t], cols[:, t, GA2:GA2 + 1], None, ALU.mult))
            n_fold = chained[0]

            def spread_x(j):
                b = j.mod(4)
                dve.wait_ge(tm_in[b], 16 * j.uses(4) + 16)
                if not (isinstance(j.u, int) and j.u == 0):
                    dve.wait_ge(tr_done, j.val(1, -3))
                src = strided(tm[:, b, 0, 0:1], [[C, TK], [TK * C, 2], [1, C]])
                dst = strided(tz[:, b, 0, 0:1], [[128, TK], [HI, 2], [1, C]])
                dve.tensor_copy(dst, src).then_inc(tz_done, 1)

            for c in range(UN):
                spread_x(Step(0, c))
            with dve.Fori(1, STEPS // UN) as u:
                for c in range(UN):
                    spread_x(Step(u, c))
            for b in range(4):
                dve.wait_ge(cm_out[b], 16 * STEPS // 4)

            for t in range(NPH):
                s = PH[t]["shift"]

                def scores(j, p):
                    dve.wait_ge(s_mm, gv(t, j, P, p + 1))
                    if s:
                        last = (j.val(1, 0) % G + 1) // G
                        kind = 2 * last + (1 if p == P - 1 else 0)
                        bi = strided(bias[:, t, bass.ds(kind, 1), 0:1], [[1, HN]])
                    else:
                        bi = bias[:, t, 0]
                    if p % 2 == 0 and not (isinstance(j.u, int) and j.c == 0 and t == 0):
                        dve.wait_ge(exp_done, gv(t, j, 4, p // 2 - 3))
                    dve.tensor_tensor(strided(S[:, p, 0, 0:1], [[1, HN]]), pS[0:M2, 0:HN], bi, ALU.add)\
                       .then_inc(s_done, 1)

                def group(q):
                    return strided(S[:, 2 * q, 0, 0:1], [[N, 2 * HEADS], [1, N]])

                def maxima(j, q):
                    dve.wait_ge(s_done, gv(t, j, P, 2 * q + 2))
                    dve.tensor_reduce(mx[:, 2 * HEADS * q:2 * HEADS * (q + 1)], group(q), AX.X, ALU.max)\
                       .then_inc(mx_done, 1)

                def less_maxima(j, q):
                    dve.wait_ge(mx_done, gv(t, j, 4, q + 1))
                    mb = strided(mx[:, 2 * HEADS * q:2 * HEADS * q + 1], [[1, 2 * HEADS], [0, N]])
                    dve.tensor_tensor(group(q), group(q), mb, ALU.subtract).then_inc(sub_done, 1)

                def sums(j, q):
                    dve.wait_ge(exp_done, gv(t, j, 4, q + 1))
                    e = strided(E[:, j.mod(2), 2 * q, 0, 0:1], [[HI, 2 * HEADS], [1, N]])
                    dve.tensor_reduce(sm[:, 2 * HEADS * q:2 * HEADS * (q + 1)], e, AX.X, ALU.add)\
                       .then_inc(sum_done, 1)

                def inverse_sums(j, q):
                    h = slice(2 * HEADS * q, 2 * HEADS * (q + 1))
                    dve.wait_ge(sum_done, gv(t, j, 4, q + 1))
                    dve.reciprocal(rs[:, j.mod(2), h], sm[:, h]).then_inc(rcp_done, 1)

                def normal1(j):
                    dve.wait_ge(rs1_done, gv(t, j, 1, 1))

                    def windows(p0, n, j0, c0, w):
                        src = [[WIN, n], [W, WIN], [1, w]]
                        return dve.tensor_tensor(
                            strided(xn1[:, p0, 0, j0:j0 + 1], [[N, n], [WIN, WIN], [1, w]]),
                            strided(pA0[0:R, c0:c0 + 1], src), strided(rs1[:, c0:c0 + 1], src), ALU.mult)

                    if s:
                        windows(0, P - 1, 0, s, WIN)
                        windows(P - 1, 1, 0, W - WIN + s, WIN - s)
                        ins = windows(P - 1, 1, WIN - s, 0, s)
                    else:
                        ins = windows(0, P, 0, 0, WIN)
                    ins.then_inc(xn1_done, 1)

                def evac_q(j):
                    dve.wait_ge(q_mm, gv(t, j, 1, 1))
                    for r in (0, HI):
                        src = pA1[r:r + C, 0:TOK].rearrange("p (a n) -> p a n", n=N)
                        ins = dve.tensor_scalar(Qbd[r:r + C, j.mod(2), :, r:r + N], src, cols[r:r + C, t, BQ:BQ + 1], None, ALU.add)
                    ins.then_inc(q_done, 1)

                def evac_v(j, half):
                    dve.wait_ge(v_mm, gv(t, j, 2, half + 1))
                    src_bank = (pA1, pA0)[half]
                    for odd in range(2):
                        src = strided(src_bank[0:N, odd * D:odd * D + 1], [[C, P], [2 * D, HP], [1, D]])
                        dst = strided(V2[HI * odd:HI * odd + N, j.mod(4), half * P, odd * D:odd * D + 1],
                                      [[VC, P], [C + 2 * D, HP], [1, D]])
                        ins = dve.tensor_copy(dst, src)
                    ins.then_inc(v_done, 1)

                def residual1(j):
                    dve.wait_ge(proj_mm, gv(t, j, 1, 1))
                    if not (isinstance(j.u, int) and j.c < 2 and t == 0):
                        dve.wait_ge(x2_done, gv(t, j, 1, -1))
                    to = x1[:, j.mod(2)]
                    y = pD0[0:R, 0:TOK].rearrange("p (r c) -> p r c", r=WIN)
                    x = xin[:, j.mod(4)].rearrange("p (r c) -> p r c", r=WIN)
                    bp = cols[:, t, BP:BP + 1]
                    ins = dve.scalar_tensor_tensor(to[:, :, s:W], y[:, :, 0:W - s], bp, x[:, :, s:W], ALU.add, ALU.add)
                    if s:
                        ins = dve.scalar_tensor_tensor(to[:, :, 0:s], y[:, :, W - s:W], bp, x[:, :, 0:s],
                                                       ALU.add, ALU.add)
                    ins.then_inc(x1_done, 1)

                def normal2(j):
                    dve.wait_ge(rs2_done, gv(t, j, 1, 1))
                    dve.tensor_tensor(xn2[:, :], pD1[0:R, 0:TOK], rs2[:, :], ALU.mult).then_inc(xn2_done, 1)

                def residual2(j):
                    b = j.mod(2)
                    dve.wait_ge(fc2_mm, gv(t, j, 1, 1))
                    if not (isinstance(j.u, int) and j.c < 2):
                        dve.wait_ge(out_st[b], j.uses(2) * 32 + t * 32 * STEPS // 2)
                    dve.wait_ge(x1_done, gv(t, j, 1, 1))
                    dve.scalar_tensor_tensor(xout[:, b], pD1[0:R, 0:TOK], cols[:, t, B2:B2 + 1],
                                             x1[:, j.mod(2)].rearrange("p r c -> p (r c)"), ALU.add, ALU.add)\
                       .then_inc(x2_done, 1)

                def iteration(a, b, c, d, e):
                    for p in range(P):
                        if b:
                            scores(b, p)
                        if p % 2:
                            q = p // 2
                            j, k = (b, q - 1) if q else (c, 3)
                            if b:
                                maxima(b, q)
                            if j:
                                sums(j, k)
                            if b:
                                less_maxima(b, q)
                            if j:
                                inverse_sums(j, k)
                        if p == 0 and b:
                            evac_v(b, 0)
                            evac_v(b, 1)
                        if p == 2 and e:
                            normal2(e)
                        if p == 4 and a:
                            normal1(a)
                        if p == 6:
                            if a:
                                evac_q(a)
                            if d:
                                residual1(d)
                        if p == 7 and e:
                            residual2(e)

                sweep(dve, t, iteration)

            def gather_tm(j):
                b = j.mod(4)
                dve.wait_ge(tr2_done, j.val(1, 1))
                if not (isinstance(j.u, int) and j.u == 0):
                    dve.wait_ge(to_out[b], 16 * j.uses(4))
                src = strided(bank[j.mod(2)][0:TP, 0:1], [[R, TK], [HI, 2], [1, C]])
                dst = strided(tm[:, b, 0, 0:1], [[C, TK], [TK * C, 2], [1, C]])
                dve.tensor_copy(dst, src).then_inc(to_done, 1)

            for c in range(UN):
                gather_tm(Step(0, c))
            with dve.Fori(1, STEPS // UN) as u:
                for c in range(UN):
                    gather_tm(Step(u, c))

        @block.tensor
        def _(pe):
            mm = pe.matmul
            pe.wait_ge(const_in, 16 * len(consts))
            pe.wait_ge(par_in, 16 * len(par))
            for k, (_, ts_) in enumerate(TABLES):
                pe.wait_ge(onehot, k + 1)
                for t in ts_:
                    for r in (0, HI):
                        for m in range(N):
                            o = bank[2 + t][r:r + N, HEADS * m:HEADS * (m + 1)]
                            mm(o, strided(oh_lo[:, m:m + 1], [[N, N]]), tab[:, t, 0], start=True, stop=False)
                            last = mm(o, strided(oh_hi[:, m:m + 1], [[N, N]]), tab[:, t, 1], start=False, stop=True)
                    last.then_inc(tab_mm, 1)
            for t in range(NPH):
                o = 8 * t
                be1, be2 = cols[:, t, BE1:BE1 + 1], cols[:, t, BE2:BE2 + 1]
                for i, w in enumerate((wq, wk, wvr)):
                    mm(bank[6][0:R, o + i:o + i + 1], w[:, t], be1, start=True, stop=True)
                for k in range(3):
                    last = mm(bank[6][:, o + 3 + k:o + 4 + k], w1[:, t, k], be2, start=True, stop=True)
                last.then_inc(bias_mm, 1)

            def transpose_x(j):
                b = j.mod(4)
                pe.wait_ge(tz_done, j.val(1, 1))
                if not (isinstance(j.u, int) and j.c < 2 and j.u == 0):
                    pe.wait_ge(cm_done, j.val(1, -1))
                for k in range(TK):
                    last = pe.transpose(bank[j.mod(2)][0:R, k * TP:(k + 1) * TP], tz[:, b, k, 0:R], ident[0:TP, 0:TP])
                last.then_inc(tr_done, 1)

            for c in range(UN):
                transpose_x(Step(0, c))
            with pe.Fori(1, STEPS // UN) as u:
                for c in range(UN):
                    transpose_x(Step(u, c))
            pe.wait_ge(cm_done, STEPS)

            for t in range(NPH):
                s = PH[t]["shift"]

                def first(j):
                    return isinstance(j.u, int) and j.c == 0

                def transposes(j, p):
                    if p % 2 == 0:
                        pe.wait_ge(norm_done, gv(t, j, 4, p // 2 + 1))
                    if not (first(j) and t == 0 and p == 0):
                        pe.wait_ge(et_done, gv(t, j, P, p))
                    for k in range(HP):
                        last = pe.transpose(pT[0:M2, k * M2:(k + 1) * M2],
                                            strided(E[:, j.mod(2), p, 2 * k, 0:1], [[1, M2]]), ident[0:M2, 0:M2])
                    last.then_inc(tr_mm, 1)

                def scores(j, p):
                    if p == 0:
                        pe.wait_ge(q_done, gv(t, j, 1, 1))
                    if p % (P // 2) == 0:
                        pe.wait_ge(kbd_done, gv(t, j, 2, 1 + 2 * p // P))
                    if not (first(j) and t == 0 and p == 0):
                        pe.wait_ge(s_done, gv(t, j, P, p))
                    mm(pS[0:M2, 0:HN], Qbd[:, j.mod(2), p, 0:M2],
                       strided(Kbd[:, j.mod(2), p, 0, 0:1], [[1, HN]]), start=True, stop=True).then_inc(s_mm, 1)

                def values(j, p):
                    pe.wait_ge(et_done, gv(t, j, P, p + 1))
                    if p == 0:
                        pe.wait_ge(v_done, gv(t, j, 2, 2))
                        if not (first(j) and t == 0):
                            pe.wait_ge(oT_done, gv(t, j, 1, 0))
                    for w in range(2):
                        for k in range(HP):
                            last = mm(pO[w][0:C, N * p:N * (p + 1)],
                                      V2[:, j.mod(4), 2 * p + w, C * k:C * (k + 1)],
                                      ET[:, p % 2, k, HI * w:HI * w + N], start=(k == 0), stop=(k == HP - 1))
                    last.then_inc(pv_mm, 1)

                def center1(j):
                    pe.wait_ge(xin_in[j.mod(4)], j.uses(4) * 32 + 32 + t * 32 * STEPS // 4)
                    if not (first(j) and t == 0):
                        pe.wait_ge(v_done, gv(t, j, 2, 0))
                    mm(pA0[0:R, 0:TOK], center[:, :], xin[:, j.mod(4)], start=True, stop=True).then_inc(ctr1_mm, 1)

                def var1(j):
                    pe.wait_ge(sq1_done, gv(t, j, 1, 1))
                    mm(pA1[0:R, 0:TOK], mean[:, :], sq1[:, :], start=True, stop=True).then_inc(var1_mm, 1)

                def query_key(j):
                    pe.wait_ge(xn1_done, gv(t, j, 1, 1))
                    mm(pA1[0:R, 0:TOK], wq[:, t], flat(xn1), start=True, stop=True).then_inc(q_mm, 1)
                    mm(pA0[0:R, 0:TOK], wk[:, t], flat(xn1), start=True, stop=True).then_inc(k_mm, 1)

                def value(j, half):
                    pe.wait_ge((q_done, kT_done)[half], gv(t, j, 1, 1))
                    for i in range(P // 2):
                        x = strided(xn1[:, half * P // 2 + i, 0, 0:1], [[1, N]])
                        last = mm((pA1, pA0)[half][0:N, 2 * C * i:2 * C * (i + 1)], x,
                                  wv[:, t], start=True, stop=True)
                    last.then_inc(v_mm, 1)

                def project(j):
                    pe.wait_ge(oT_done, gv(t, j, 1, 1))
                    if not (first(j) and t == 0):
                        pe.wait_ge(gelu_done, gv(t, j, 3, 0))
                    rolled = strided(oT[:, 0, 0:1], [[WIN, WIN], [N, P], [1, WIN]])
                    mm(pD0[0:R, 0:TOK], wp[:, t], rolled, start=True, stop=True).then_inc(proj_mm, 1)

                def center2(j):
                    pe.wait_ge(x1_done, gv(t, j, 1, 1))
                    if not (first(j) and t == 0):
                        pe.wait_ge(x2_done, gv(t, j, 1, 0))
                    mm(pD1[0:R, 0:TOK], center[:, :], x1[:, j.mod(2)].rearrange("p r c -> p (r c)"),
                       start=True, stop=True).then_inc(ctr2_mm, 1)

                def var2(j):
                    pe.wait_ge(sq2_done, gv(t, j, 1, 1))
                    mm(pD0[0:R, 0:TOK], mean[:, :], sq2[:, :], start=True, stop=True).then_inc(var2_mm, 1)

                def up(j, k):
                    if k == 0:
                        pe.wait_ge(xn2_done, gv(t, j, 1, 1))
                    if k == 2:
                        pe.wait_ge(gelu_done, gv(t, j, 3, 1))
                    mm((pD0, pD1, pD0)[k][:, 0:TOK], w1[:, t, k], xn2[:, :], start=True, stop=True).then_inc(fc1_mm, 1)

                def down(j):
                    for k in range(3):
                        pe.wait_ge(gelu_done, gv(t, j, 3, max(k, 1) + 1))
                        last = mm(pD1[0:R, 0:TOK], w2[:, t, k], hT[:, k], start=(k == 0), stop=(k == 2))
                    last.then_inc(fc2_mm, 1)

                def iteration(a, b, c, d, e):
                    for p in range(P):
                        if c:
                            transposes(c, p)
                        if b:
                            scores(b, p)
                        if p == 0 and e:
                            center2(e)
                        if p == 1:
                            if e:
                                var2(e)
                            if a:
                                center1(a)
                        if p == 2 and a:
                            var1(a)
                        if p == 3 and e:
                            up(e, 0)
                            up(e, 1)
                        if p == 4 and e:
                            up(e, 2)
                        if p == 5:
                            if a:
                                query_key(a)
                            if d:
                                project(d)
                        if p == 6 and e:
                            down(e)
                        if p == 7 and a:
                            value(a, 0)
                            value(a, 1)
                        if c:
                            values(c, p)

                sweep(pe, t, iteration)

            pe.wait_ge(x2_done, NPH * STEPS)

            def transpose_out(j):
                b = j.mod(4)
                pe.wait_ge(cm_in[b], 16 * j.uses(4) + 16)
                if not (isinstance(j.u, int) and j.c < 2 and j.u == 0):
                    pe.wait_ge(to_done, j.val(1, -1))
                for k in range(TK):
                    last = pe.transpose(bank[j.mod(2)][0:TP, k * R:(k + 1) * R],
                                        strided(cm[:, b, k:k + 1], [[TK, TP]]), ident[0:R, 0:R])
                last.then_inc(tr2_done, 1)

            for c in range(UN):
                transpose_out(Step(0, c))
            with pe.Fori(1, STEPS // UN) as u:
                for c in range(UN):
                    transpose_out(Step(u, c))


def constants():
    eye = np.eye(128, dtype=np.float32)
    center = np.zeros((R, R), np.float32)
    mean = np.zeros((R, R), np.float32)
    headmask = np.zeros((R, HEADS), np.float32)
    for r in (0, HI):
        mean[r:r + C, r:r + C] = 1.0 / C
        center[r:r + C, r:r + C] = np.eye(C) - 1.0 / C
        for h in range(HEADS):
            headmask[r + D * h:r + D * (h + 1), h] = 1.0
    kcol = np.stack([np.arange(128), np.arange(128) + 128], 1).astype(np.float32)
    i, j = np.divmod(np.arange(N), WIN)
    col = (j[:, None] < WIN - SHIFT) != (j[None, :] < WIN - SHIFT)
    row = (i[:, None] < WIN - SHIFT) != (i[None, :] < WIN - SHIFT)
    regions = np.stack([col, row, col | row], 1).astype(np.float32)
    rel = ((i[:, None] - i[None, :] + WIN - 1) * (2 * WIN - 1) + j[:, None] - j[None, :] + WIN - 1)
    return dict(ident=eye, center=center, mean=mean, headmask=headmask, kcol=kcol, regions=regions,
                rel_const=rel.reshape(-1).astype(np.int32))


def kernel(**inputs):
    import concourse.bacc as bacc
    from concourse.bass_utils import run_bass_kernel_spmd

    nc = bacc.Bacc("TRN2", target_bir_lowering=False, num_devices=1)
    arrays, aps = {}, {}
    for name, a in {**inputs, **constants()}.items():
        a = np.ascontiguousarray(a)
        arrays[f"in_{name}"] = a
        aps[name] = nc.dram_tensor(f"in_{name}", a.shape, mybir.dt.from_np(a.dtype), kind="ExternalInput").ap()
    out = nc.dram_tensor("out", (B, H, W, C), mybir.dt.float32, kind="ExternalOutput").ap()
    build(nc, aps, out)
    r = run_bass_kernel_spmd(nc, [arrays], core_ids=[0])
    return r.results[0]["out"]
```

```python
from contextlib import ExitStack

import numpy as np

import concourse.bass as bass
from concourse import mybir

B, H, W, C = 32, 56, 56, 48
HEADS, WIN, SHIFT = 6, 7, 3
D = C // HEADS
N = WIN * WIN
HID = 4 * C
REL = (2 * WIN - 1) ** 2
EPS = 1e-5

HI = 64
R = HI + C
M2 = HI + N
PAIRS = B // 2
G = H // WIN
STEPS = PAIRS * G
TOK = WIN * W
P = W // WIN
HN = HEADS * N
IMG = H * W
TP, TK = 98, 4
NPH = 3
UN = 8
XB = 8
HP = HEADS // 2
VC = HP * C


class Step:

    def __init__(self, u, c, t=0):
        self.u, self.c, self.t = u, c, t

    def val(self, scale, add):
        return self.u * (UN * scale) + (self.c * scale + add)

    def uses(self, of):
        return self.u * (UN // of) + self.c // of

    def last(self):
        return isinstance(self.u, int) and self.t == NPH - 1 and UN * self.u + self.c == STEPS - 1

    def next(self):
        if isinstance(self.u, int) and UN * self.u + self.c == STEPS - 1:
            return Step(0, 0, self.t + 1)
        return Step(self.u, self.c + 1, self.t)

    def before(self, n):
        return isinstance(self.u, int) and self.t == 0 and UN * self.u + self.c < n

    def mod(self, of):
        return self.c % of


def build(nc, A, out):
    fp32, i32, fp32r = mybir.dt.float32, mybir.dt.int32, mybir.dt.float32r
    ALU, ACT, AX = mybir.AluOpType, mybir.ActivationFunctionType, mybir.AxisListType
    ctx = ExitStack()
    with ctx:
        def sb(name, shape, dt=fp32):
            return ctx.enter_context(nc.sbuf_tensor(name, shape, dt))

        def sem(name):
            return ctx.enter_context(nc.semaphore(name))

        L0, L1 = "L0_conv_", "L1_conv_"
        mlp1 = dict(g1=L1 + "ln1_g", b1=L1 + "ln1_b", g2=L1 + "ln2_g", b2=L1 + "ln2_b",
                    w1=L1 + "mlp_w1", c1=L1 + "mlp_b1", w2=L1 + "mlp_w2", c2=L1 + "mlp_b2",
                    gelu=ACT.Gelu_apprx_tanh, index=L1 + "rel_index")
        PH = [
            dict(g1=L0 + "norm1_w", b1=L0 + "norm1_b", g2=L0 + "norm2_w", b2=L0 + "norm2_b",
                 w1=L0 + "fc1_w", c1=L0 + "fc1_b", w2=L0 + "fc2_w", c2=L0 + "fc2_b",
                 wqkv=L0 + "qkv_w", bqkv=L0 + "qkv_b", wp=L0 + "proj_w", bp=L0 + "proj_b",
                 table=L0 + "rpb_table", index="rel_const", gelu=ACT.Gelu, shift=SHIFT, neg=-100.0),
            dict(mlp1, wqkv=L1 + "w_qkv_w", bqkv=L1 + "w_qkv_b", wp=L1 + "w_proj_w",
                 bp=L1 + "w_proj_b", table=L1 + "w_rel", shift=0, neg=0.0),
            dict(mlp1, wqkv=L1 + "s_qkv_w", bqkv=L1 + "s_qkv_b", wp=L1 + "s_proj_w",
                 bp=L1 + "s_proj_b", table=L1 + "s_rel", shift=SHIFT, neg=-1e9),
        ]
        assert len(PH) == NPH

        scratch = [nc.dram_tensor(f"xT{k}", (PAIRS, R, IMG), fp32, kind="Internal").ap()
                   for k in range(NPH + 1)]
        x_tm = A["x"].rearrange("(P i) h w c -> P i (h w c)", i=2)\
                     .rearrange("P i (g p e) -> P g p i e", g=G, p=TP)
        o_tm = out.rearrange("(P i) h w c -> P i (h w c)", i=2)\
                  .rearrange("P i (g p e) -> P g p i e", g=G, p=TP)

        ident = sb("ident", [128, 128])
        center = sb("center", [R, R])
        ones = sb("ones", [R, R])
        headmask = sb("headmask", [R, HEADS])
        eps = sb("eps", [R, 1])
        kcol = sb("kcol", [128, 2])
        regions = sb("regions", [M2, 3, N])
        wq = sb("wq", [R, NPH, R])
        wk = sb("wk", [R, NPH, R])
        wq_hi, wq_lo = sb("wq_hi", [R, NPH, R], fp32r), sb("wq_lo", [R, NPH, R], fp32r)
        wk_hi, wk_lo = sb("wk_hi", [R, NPH, R], fp32r), sb("wk_lo", [R, NPH, R], fp32r)
        wvr = sb("wvr", [R, NPH, R])
        wv = sb("wv", [R, NPH, 2 * C])
        wp = sb("wp", [R, NPH, R])
        w1 = sb("w1", [R, NPH, 3, 128])
        w1_hi, w1_lo = sb("w1_hi", [R, NPH, 3, 128], fp32r), sb("w1_lo", [R, NPH, 3, 128], fp32r)
        center_hi = sb("center_hi", [R, R], fp32r)
        w2 = sb("w2", [128, NPH, 3, R])
        GA1, BE1, GA2, BE2, BQ, BK, BV, BP, B2 = range(9)
        cols = sb("cols", [R, NPH, 9])
        b1c = sb("b1c", [128, NPH, 3])
        bias = sb("bias", [M2, NPH, 4, HN])

        Qbd = sb("Qbd", [R, 2, P, 128])
        V2 = sb("V2", [M2, 4, 2 * P, VC])
        E = sb("E", [M2, 2, P, HEADS, HI])
        oT = sb("oT", [R, P, N])

        with ExitStack() as early:
            def tmp(name, shape, dt=fp32):
                return early.enter_context(nc.sbuf_tensor(name, shape, dt))

            tm = tmp("tm", [TP, 4, 2, TK * C])
            tz = tmp("tz", [TP, 4, TK, 128])
            cm = tmp("cm", [R, 4, TOK])
            idx_i = tmp("idx_i", [128, N * N], i32)
            idx_f = tmp("idx_f", [128, N * N])
            oh_lo = tmp("oh_lo", [128, N * N])
            oh_hi = tmp("oh_hi", [128, N * N])
            tab = tmp("tab", [128, NPH, 2, HEADS])
            neg = tmp("neg", [M2, NPH, 3, N])

        xin = sb("xin", [R, XB, TOK])
        x_hi, x_lo = sb("x_hi", [R, TOK], fp32r), sb("x_lo", [R, TOK], fp32r)
        x1_hi, x1_lo = sb("x1_hi", [R, TOK], fp32r), sb("x1_lo", [R, TOK], fp32r)
        xn1_hi, xn1_lo = sb("xn1_hi", [R, TOK], fp32r), sb("xn1_lo", [R, TOK], fp32r)
        xn2_hi, xn2_lo = sb("xn2_hi", [R, TOK], fp32r), sb("xn2_lo", [R, TOK], fp32r)
        sq1 = sb("sq1", [R, TOK])
        va1 = sb("va1", [R, TOK])
        rs1 = sb("rs1", [R, TOK])
        xn1 = sb("xn1", [R, P, WIN, WIN])
        KT = sb("KT", [R, P, N])
        Kbd = sb("Kbd", [R, 2, P, HEADS, N])
        S = sb("S", [M2, P, HEADS, N])
        mx = sb("mx", [M2, P * HEADS])
        sm = sb("sm", [M2, P * HEADS])
        rs = sb("rs", [M2, 2, P * HEADS])
        ET = sb("ET", [M2, 2, HP, M2])
        x1 = sb("x1", [R, 2, WIN, W])
        sq2 = sb("sq2", [R, TOK])
        va2 = sb("va2", [R, TOK])
        rs2 = sb("rs2", [R, TOK])
        xn2 = sb("xn2", [R, TOK])
        hT = sb("hT", [128, 3, TOK])
        xout = sb("xout", [R, 2, TOK])

        bank = [ctx.enter_context(nc.psum_tensor(f"bank{k}", [128, 512], fp32)) for k in range(8)]
        pS, pT, pO0, pO1, pA0, pA1, pD0, pD1 = bank
        pO = [pO0, pO1]

        def strided(ap, dims):
            return bass.AP(ap.tensor, ap.offset, [list(ap.ap[0])] + [list(d) for d in dims])

        zeroed = sem("zeroed")
        const_in = sem("const_in")
        par_in = sem("par_in")
        idx_in = sem("idx_in")
        onehot = sem("onehot")
        tab_mm = sem("tab_mm")
        set_up = sem("set_up")
        bias_mm = sem("bias_mm")
        fold = sem("fold")
        tm_in = [sem(f"tm_in{b}") for b in range(4)]
        tz_done, tr_done, cm_done = sem("tz_done"), sem("tr_done"), sem("cm_done")
        cm_out = [sem(f"cm_out{b}") for b in range(4)]
        cm_in = [sem(f"cm_in{b}") for b in range(4)]
        tr2_done, to_done = sem("tr2_done"), sem("to_done")
        to_out = [sem(f"to_out{b}") for b in range(4)]
        xin_in = [sem(f"xin_in{b}") for b in range(XB)]
        out_st = [sem(f"out_st{b}") for b in range(2)]
        ctr1_mm, sq1_done, var1_mm, va1_done, rs1_done, xn1_done = (
            sem(n) for n in ("ctr1_mm", "sq1_done", "var1_mm", "va1_done", "rs1_done", "xn1_done"))
        q_mm, k_mm, v_mm = sem("q_mm"), sem("k_mm"), sem("v_mm")
        q_done, kT_done = sem("q_done"), sem("kT_done")
        kbd_done, v_done = sem("kbd_done"), sem("v_done")
        s_mm, s_done = sem("s_mm"), sem("s_done")
        mx_done, sub_done, exp_done, sum_done, rcp_done, norm_done = (
            sem(n) for n in ("mx_done", "sub_done", "exp_done", "sum_done", "rcp_done", "norm_done"))
        tr_mm, et_done = sem("tr_mm"), sem("et_done")
        pv_mm = sem("pv_mm")
        oT_done, oT1_done = sem("oT_done"), sem("oT1_done")
        proj_mm, x1_done, ctr2_mm, sq2_done, var2_mm, va2_done, rs2_done, xn2_done = (
            sem(n) for n in ("proj_mm", "x1_done", "ctr2_mm", "sq2_done", "var2_mm", "va2_done",
                             "rs2_done", "xn2_done"))
        x_hi_done, xn1_hi_done, x1_hi_done, xn2_hi_done = (
            sem(n + "_hi_done") for n in ("x", "xn1", "x1", "xn2"))
        x_lo_done, xn1_lo_done, x1_lo_done, xn2_lo_done = (
            sem(n + "_lo_done") for n in ("x", "xn1", "x1", "xn2"))
        fc1_mm, gelu_done = sem("fc1_mm"), sem("gelu_done")
        fc2_mm, x2_done = sem("fc2_mm"), sem("x2_done")

        def col(t, j, v, o=0):
            return [(cols[r:r + C, t, j:j + 1], v[o:o + C].rearrange("(c a) -> c a", a=1)) for r in (0, HI)]

        def diag(tile, t, src):
            return [(tile[r:r + C, t, r:r + C], src) for r in (0, HI)]

        par = []
        for t, ph in enumerate(PH):
            wqkv, bqkv = A[ph["wqkv"]], A[ph["bqkv"]]
            for k, tile in enumerate((wq, wk, wvr)):
                par += diag(tile, t, wqkv[:, k * C:(k + 1) * C])
            par += diag(wp, t, A[ph["wp"]])
            for j, v, o in ((GA1, ph["g1"], 0), (BE1, ph["b1"], 0), (GA2, ph["g2"], 0), (BE2, ph["b2"], 0),
                            (BQ, ph["bqkv"], 0), (BK, ph["bqkv"], C), (BV, ph["bqkv"], 2 * C),
                            (BP, ph["bp"], 0), (B2, ph["c2"], 0)):
                par += col(t, j, A[v], o)
            for k, lo, r, h0, n in ((0, 0, 0, 0, 128), (1, 0, 0, 128, 64), (1, 64, HI, 0, 64), (2, 0, HI, 64, 128)):
                par.append((w1[r:r + C, t, k, lo:lo + n], A[ph["w1"]][:, h0:h0 + n]))
                par.append((w2[lo:lo + n, t, k, r:r + C], A[ph["w2"]][h0:h0 + n, :]))
                par.append((b1c[lo:lo + n, t, k:k + 1], A[ph["c1"]][h0:h0 + n].rearrange("(c a) -> c a", a=1)))
            par.append((tab[:, t, 0, :], A[ph["table"]][0:128, :]))
            par.append((tab[0:REL - 128, t, 1, :], A[ph["table"]][128:REL, :]))
        consts = [(ident[:, :], A["ident"]), (center[:, :], A["center"]), (ones[:, :], A["ones"]),
                  (headmask[:, :], A["headmask"]), (kcol[:, :], A["kcol"]),
                  (regions[0:N, :, :], A["regions"]), (regions[HI:M2, :, :], A["regions"])]
        TABLES = [("rel_const", [0]), (L1 + "rel_index", [1, 2])]
        CLEARED = [tz, wq, wk, wvr, wp, w1, w2, cols, b1c, tab, bias, neg, Qbd, V2, E, oT]

        def flat(tile):
            ap = tile[:]
            n = 1
            for d in ap.shape[1:]:
                n *= d
            return strided(ap, [[1, n]])

        block = ctx.enter_context(nc.Block())

        def sweep(eng, iteration):
            ahead = (1, 0, -1, -2, -3)
            begin = 5
            full = (STEPS - begin - 2) // UN

            def peeled(i):
                iteration(*(Step(0, (i + k) % STEPS, (i + k) // STEPS) if 0 <= i + k < NPH * STEPS else None
                            for k in ahead))

            for i in range(-1, begin):
                peeled(i)
            for t in range(NPH):
                with eng.Fori(0, full) as u:
                    for k in range(UN):
                        iteration(*(Step(u, begin + k + o, t) for o in ahead))
                for i in range(begin + UN * full, STEPS + (begin if t < NPH - 1 else 3)):
                    peeled(i + t * STEPS)

        SPLIT = WIN - SHIFT

        def piece(k, j, part):
            s = PH[j.t]["shift"]
            pair, g = j.val(1, 0) // G, j.val(1, 0) % G
            if part == 0:
                return scratch[k][bass.ds(pair, 1), :, bass.ds(g * TOK + s * W, SPLIT * W)]\
                    .rearrange("a r n -> (a r) n")
            if s:
                g, at = (j.val(1, 1)) % G, 0
            else:
                at = SPLIT * W
            return scratch[k][bass.ds(pair, 1), :, bass.ds(g * TOK + at, SHIFT * W)]\
                .rearrange("a r n -> (a r) n")

        def of_step(dram, j):
            pair, g = j.val(1, 0) // G, j.val(1, 0) % G
            return dram[bass.ds(pair, 1), bass.ds(g, 1)].rearrange("a b p i e -> (a b p) i e")

        def mine(part):
            return slice(0, SPLIT * W) if part == 0 else slice(SPLIT * W, TOK)

        def gv(j, scale=1, add=0):
            return j.val(scale, add + j.t * STEPS * scale)

        @block.sync
        def _(sp):
            for to, of in consts:
                sp.dma_start(to, of).then_inc(const_in, 16)

            def load_x(j):
                b = j.mod(4)
                if not j.before(4):
                    sp.wait_ge(tz_done, j.val(1, -3))
                sp.dma_start(tm[:, b], of_step(x_tm, j))\
                  .then_inc(tm_in[b], 16)

            for c in range(4):
                load_x(Step(0, c))
            def load_index(k):
                index = A[TABLES[k][0]]
                if len(index.shape) == 2:
                    index = index.rearrange("a b -> (a b)")
                sp.dma_start(idx_i[:, :], index.rearrange("(a n) -> a n", a=1).to_broadcast([128, N * N]))\
                  .then_inc(idx_in, 16)

            load_index(0)
            for c in range(4, UN):
                load_x(Step(0, c))
            with sp.Fori(1, STEPS // UN) as u:
                for c in range(UN):
                    load_x(Step(u, c))
            sp.wait_ge(onehot, 1)
            load_index(1)
            for b in range(4):
                sp.wait_ge(cm_out[b], 16 * STEPS // 4)
            sp.wait_ge(set_up, 1)

            def load(j):
                b = j.mod(XB)
                if not j.before(XB):
                    sp.wait_ge(x1_done, gv(j, 1, 1 - XB))
                if j.t:
                    done = (j.val(1, 0) // G) * G + (G + (j.t - 1) * STEPS)
                    for k in range(2):
                        sp.wait_ge(out_st[k], done * 16)
                for part in range(2):
                    sp.dma_start(xin[:, b, mine(part)], piece(j.t, j, part)).then_inc(xin_in[b], 16)

            def store(j):
                t = j.t
                b = j.mod(2)
                sp.wait_ge(x2_done, gv(j, 1, 1))
                for part in range(2):
                    sp.dma_start(piece(j.t + 1, j, part), xout[:, b, mine(part)]).then_inc(out_st[b], 16)

            load(Step(0, 0))
            load(Step(0, 1))

            def iteration(a, b, c, d, e):
                if a and not a.last() and not a.next().last():
                    load(a.next().next())
                if e:
                    store(e)

            sweep(sp, iteration)

            for b in range(2):
                sp.wait_ge(out_st[b], 32 * NPH * STEPS // 2)

            def load_cm(j):
                b = j.mod(4)
                if not j.before(4):
                    sp.wait_ge(tr2_done, j.val(1, -3))
                sp.dma_start(cm[:, b], scratch[NPH][bass.ds(j.val(1, 0) // G, 1), :, bass.ds((j.val(1, 0) % G) * TOK, TOK)]
                             .rearrange("a r n -> (a r) n")).then_inc(cm_in[b], 16)

            for c in range(UN):
                load_cm(Step(0, c))
            with sp.Fori(1, STEPS // UN) as u:
                for c in range(UN):
                    load_cm(Step(u, c))

        @block.gpsimd
        def _(pool):
            for tile in CLEARED:
                pool.memset(flat(tile), 0.0).then_inc(zeroed, 1)
            pool.memset(eps[:, :], EPS).then_inc(zeroed, 1)

            def store_cm(j):
                b = j.mod(4)
                pool.wait_ge(cm_done, j.val(1, 1))
                pool.dma_start(scratch[0][bass.ds(j.val(1, 0) // G, 1), :, bass.ds((j.val(1, 0) % G) * TOK, TOK)]
                               .rearrange("a r n -> (a r) n"), cm[:, b]).then_inc(cm_out[b], 16)

            for c in range(UN):
                store_cm(Step(0, c))
            with pool.Fori(1, STEPS // UN) as u:
                for c in range(UN):
                    store_cm(Step(u, c))

            def norm(j, q):
                b = j.mod(2)
                pool.wait_ge(rcp_done, gv(j, 4, q + 1))
                e = strided(E[:, b, 2 * q, 0, 0:1], [[HI, 2 * HEADS], [1, N]])
                r = strided(rs[:, b, 2 * HEADS * q:2 * HEADS * q + 1], [[1, 2 * HEADS], [0, N]])
                pool.tensor_tensor(e, e, r, ALU.mult).then_inc(norm_done, 1)

            def spread_k(j, half):
                if half == 0:
                    pool.wait_ge(kT_done, gv(j, 1, 1))
                p0 = half * P // 2
                k = strided(KT[:, p0, 0:1], [[N, P // 2], [0, HEADS], [1, N]])
                m = strided(headmask[:, 0:1], [[0, P // 2], [1, HEADS], [0, N]])
                pool.tensor_tensor(Kbd[:, j.mod(2), p0:p0 + P // 2], k, m, ALU.mult).then_inc(kbd_done, 1)

            def low(j, x, hi, lo, hi_done, done):
                pool.wait_ge(hi_done, gv(j, 1, 1))
                pool.tensor_tensor(lo[:, :], x, hi[:, :].bitcast(fp32), ALU.subtract).then_inc(done, 1)

            def iteration(a, b, c, d, e):
                if a:
                    low(a, xin[:, a.mod(XB)], x_hi, x_lo, x_hi_done, x_lo_done)
                if c:
                    norm(c, 2)
                    norm(c, 3)
                if b:
                    norm(b, 0)
                if a:
                    spread_k(a, 0)
                if b:
                    norm(b, 1)
                if d:
                    low(d, x1[:, d.mod(2)].rearrange("p r c -> p (r c)"), x1_hi, x1_lo, x1_hi_done, x1_lo_done)
                if a:
                    spread_k(a, 1)

            sweep(pool, iteration)

        @block.scalar
        def _(act):
            act.wait_ge(zeroed, len(CLEARED) + 1)
            for to, of in par:
                act.dma_start(to, of).then_inc(par_in, 16)

            act.preload_act_table_set("natural_log_exp_and_others")
            def evac_et(j, p):
                act.wait_ge(tr_mm, gv(j, P, p + 1))
                act.activation(flat3(ET[:, p % 2]), pT[0:M2, 0:HP * M2], ACT.Copy).then_inc(et_done, 1)

            def flat3(ap):
                return strided(ap, [[1, HP * M2]])

            def evac_o(j):
                act.wait_ge(pv_mm, gv(j, P, P))
                act.activation(strided(oT[0:C, 0, 0:1], [[1, TOK]]), pO0[0:C, 0:TOK],
                               ACT.Identity, bias=cols[0:C, j.t, BV:BV + 1]).then_inc(oT_done, 1)

            def square(j, mm, src, dst, done):
                act.wait_ge(mm, gv(j, 1, 1))
                act.activation(dst[:, :], src[0:R, 0:TOK], ACT.Square).then_inc(done, 1)

            def inverse_std(j, mm, src, va, rstd, va_done, done):
                act.wait_ge(mm, gv(j, 1, 1))
                act.activation(va[:, :], src[0:R, 0:TOK], ACT.Ln, bias=eps[:, 0:1], scale=1.0 / C ** 3).then_inc(va_done, 1)
                act.wait_ge(va_done, gv(j, 1, 1))
                act.activation(rstd[:, :], va[:, :], ACT.Exp, scale=-0.5).then_inc(done, 1)

            def exps(j, q):
                act.wait_ge(sub_done, gv(j, 4, q + 1))
                e = strided(E[:, j.mod(2), 2 * q, 0, 0:1], [[HI, 2 * HEADS], [1, N]])
                s = strided(S[:, 2 * q, 0, 0:1], [[N, 2 * HEADS], [1, N]])
                act.activation(e, s, ACT.Exp).then_inc(exp_done, 1)

            def evac_k(j):
                t = j.t
                act.wait_ge(k_mm, gv(j, 1, 1))
                act.activation(flat(KT), pA0[0:R, 0:TOK], ACT.Identity, bias=cols[:, t, BK:BK + 1]).then_inc(kT_done, 1)

            def evac_q(j):
                t = j.t
                act.wait_ge(q_mm, gv(j, 1, 1))
                for r in (0, HI):
                    src = pA1[r:r + C, 0:TOK].rearrange("p (a n) -> p a n", n=N)
                    ins = act.activation(Qbd[r:r + C, j.mod(2), :, r:r + N], src, ACT.Identity,
                                         bias=cols[r:r + C, t, BQ:BQ + 1])
                ins.then_inc(q_done, 1)

            def evac_v(j, half):
                act.wait_ge(v_mm, gv(j, 2, half + 1))
                src_bank = (pA1, pA0)[half]
                for odd in range(2):
                    src = strided(src_bank[0:N, odd * D:odd * D + 1], [[C, P], [2 * D, HP], [1, D]])
                    dst = strided(V2[HI * odd:HI * odd + N, j.mod(4), half * P, odd * D:odd * D + 1],
                                  [[VC, P], [C + 2 * D, HP], [1, D]])
                    ins = act.activation(dst, src, ACT.Copy)
                ins.then_inc(v_done, 1)

            def hidden(j, k):
                t, gelu = j.t, PH[j.t]["gelu"]
                act.wait_ge(fc1_mm, gv(j, 3, k + 1))
                act.activation(hT[:, k], (pD0, pD1, pD0)[k][:, 0:TOK], gelu, bias=b1c[:, t, k:k + 1])\
                   .then_inc(gelu_done, 1)

            def iteration(a, b, c, d, e):
                for p in range(P):
                    if c:
                        evac_et(c, p)
                    if p == 0:
                        if e:
                            square(e, ctr2_mm, pD1, sq2, sq2_done)
                        if d:
                            evac_o(d)
                        if c:
                            exps(c, 3)
                    if p == 1:
                        if a:
                            square(a, ctr1_mm, pA0, sq1, sq1_done)
                        if e:
                            inverse_std(e, var2_mm, pD0, va2, rs2, va2_done, rs2_done)
                    if p == 2:
                        if b:
                            exps(b, 0)
                        if a:
                            inverse_std(a, var1_mm, pA1, va1, rs1, va1_done, rs1_done)
                    if p == 3:
                        if e:
                            hidden(e, 0)
                            hidden(e, 1)
                    if p == 4:
                        if e:
                            hidden(e, 2)
                            act.preload_act_table_set("natural_log_exp_and_others")
                        if b:
                            exps(b, 1)
                    if p == 5:
                        if a:
                            evac_k(a)
                            evac_q(a)
                    if p == 6:
                        if b:
                            exps(b, 2)
                    if p == 7:
                        if a:
                            evac_v(a, 0)
                            evac_v(a, 1)

            sweep(act, iteration)

            def store_tm(j):
                b = j.mod(4)
                act.wait_ge(to_done, j.val(1, 1))
                act.dma_start(of_step(o_tm, j), tm[:, b])\
                   .then_inc(to_out[b], 16)

            for c in range(UN):
                store_tm(Step(0, c))
            with act.Fori(1, STEPS // UN) as u:
                for c in range(UN):
                    store_tm(Step(u, c))
            for b in range(4):
                act.wait_ge(to_out[b], 16 * STEPS // 4)

        @block.vector
        def _(dve):
            chained = [0]

            def chain(ins):
                chained[0] += 1
                ins.then_inc(fold, 1)
                dve.wait_ge(fold, chained[0])

            def spread_x(j):
                b = j.mod(4)
                dve.wait_ge(tm_in[b], 16 * j.uses(4) + 16)
                if not j.before(4):
                    dve.wait_ge(tr_done, j.val(1, -3))
                src = strided(tm[:, b, 0, 0:1], [[C, TK], [TK * C, 2], [1, C]])
                dst = strided(tz[:, b, 0, 0:1], [[128, TK], [HI, 2], [1, C]])
                dve.tensor_copy(dst, src).then_inc(tz_done, 1)

            def evac_cm(j):
                b = j.mod(4)
                dve.wait_ge(tr_done, j.val(1, 1))
                if not j.before(4):
                    dve.wait_ge(cm_out[b], j.uses(4) * 16)
                src = strided(bank[j.mod(2)][0:R, 0:1], [[1, TP], [TP, TK]])
                dve.tensor_copy(strided(cm[:, b, 0:1], [[TK, TP], [1, TK]]), src).then_inc(cm_done, 1)

            dve.wait_ge(zeroed, 1)
            for c in range(UN):
                spread_x(Step(0, c))
                if c:
                    evac_cm(Step(0, c - 1))
            with dve.Fori(1, STEPS // UN) as u:
                for c in range(UN):
                    spread_x(Step(u, c))
                    evac_cm(Step(u, c - 1))
            evac_cm(Step(0, STEPS - 1))

            dve.wait_ge(zeroed, len(CLEARED) + 1)
            dve.wait_ge(const_in, 16 * len(consts))
            for t, ph in enumerate(PH):
                for r in (0, HI):
                    chain(dve.tensor_scalar(neg[r:r + N, t], regions[r:r + N], ph["neg"], None, ALU.mult))
            tables = 0
            for k, (_, ts_) in enumerate(TABLES):
                dve.wait_ge(idx_in, 16 * (k + 1))
                chain(dve.tensor_copy(idx_f[:, :], idx_i[:, :]))
                if k:
                    dve.wait_ge(tab_mm, 1)
                dve.tensor_scalar(oh_lo[:, :], idx_f[:, :], kcol[:, 0:1], None, ALU.is_equal)
                dve.tensor_scalar(oh_hi[:, :], idx_f[:, :], kcol[:, 1:2], None, ALU.is_equal).then_inc(onehot, 1)
                for t in ts_:
                    tables += 1
                    dve.wait_ge(tab_mm, tables)
                    for r in (0, HI):
                        src = strided(bank[2 + t][r:r + N, 0:1], [[1, HEADS], [HEADS, N]])
                        chain(dve.tensor_copy(bias[r:r + N, t, 0].rearrange("p (h m) -> p h m", m=N), src))
                        for kind in range(1, 4):
                            if PH[t]["shift"]:
                                dve.tensor_tensor(
                                    bias[r:r + N, t, kind].rearrange("p (h m) -> p h m", m=N),
                                    bias[r:r + N, t, 0].rearrange("p (h m) -> p h m", m=N),
                                    strided(neg[r:r + N, t, kind - 1, 0:1], [[0, HEADS], [1, N]]), ALU.add)
            dve.wait_ge(bias_mm, NPH)
            QS = float(D) ** -0.5
            for t in range(NPH):
                m = bank[6]
                o = 8 * t
                chain(dve.tensor_tensor(cols[:, t, BQ:BV + 1], cols[:, t, BQ:BV + 1], m[0:R, o:o + 3], ALU.add))
                chain(dve.tensor_scalar(cols[:, t, BQ:BQ + 1], cols[:, t, BQ:BQ + 1], QS, None, ALU.mult))
                chain(dve.tensor_tensor(b1c[:, t], b1c[:, t], m[:, o + 3:o + 6], ALU.add))
                ga = cols[:, t, GA1:GA1 + 1]
                dve.tensor_scalar(wq[:, t], wq[:, t], ga, QS / C, ALU.mult, ALU.mult)
                dve.tensor_scalar(wk[:, t], wk[:, t], ga, 1.0 / C, ALU.mult, ALU.mult)
                dve.tensor_scalar(wv[:, t].rearrange("p (i c) -> p i c", i=2),
                                  strided(wvr[:, t, 0:1], [[HI, 2], [1, C]]), ga, 1.0 / C, ALU.mult, ALU.mult)
                chain(dve.tensor_scalar(w1[:, t], w1[:, t], cols[:, t, GA2:GA2 + 1], 1.0 / C, ALU.mult, ALU.mult))
            for w, hi, lo in ((w1, w1_hi, w1_lo), (wq, wq_hi, wq_lo), (wk, wk_hi, wk_lo)):
                chain(dve.tensor_copy(flat(hi), flat(w)))
                chain(dve.tensor_tensor(flat(lo), flat(w), flat(hi).bitcast(fp32), ALU.subtract))
            dve.tensor_copy(center_hi[:, :], center[:, :]).then_inc(set_up, 1)
            for b in range(4):
                dve.wait_ge(cm_out[b], 16 * STEPS // 4)

            def scores(j, p):
                t, s = j.t, PH[j.t]["shift"]
                dve.wait_ge(s_mm, gv(j, P, p + 1))
                if s:
                    last = (j.val(1, 0) % G + 1) // G
                    kind = 2 * last + (1 if p == P - 1 else 0)
                    bi = strided(bias[:, t, bass.ds(kind, 1), 0:1], [[1, HN]])
                else:
                    bi = bias[:, t, 0]
                if p % 2 == 0 and not (j.before(1)):
                    dve.wait_ge(exp_done, gv(j, 4, p // 2 - 3))
                dve.tensor_tensor(strided(S[:, p, 0, 0:1], [[1, HN]]), pS[0:M2, 0:HN], bi, ALU.add)\
                   .then_inc(s_done, 1)

            def group(q):
                return strided(S[:, 2 * q, 0, 0:1], [[N, 2 * HEADS], [1, N]])

            def maxima(j, q):
                dve.wait_ge(s_done, gv(j, P, 2 * q + 2))
                dve.tensor_reduce(mx[:, 2 * HEADS * q:2 * HEADS * (q + 1)], group(q), AX.X, ALU.max)\
                   .then_inc(mx_done, 1)

            def less_maxima(j, q):
                dve.wait_ge(mx_done, gv(j, 4, q + 1))
                mb = strided(mx[:, 2 * HEADS * q:2 * HEADS * q + 1], [[1, 2 * HEADS], [0, N]])
                dve.tensor_tensor(group(q), group(q), mb, ALU.subtract).then_inc(sub_done, 1)

            def evac_o(j):
                dve.wait_ge(pv_mm, gv(j, P, P))
                dve.tensor_scalar(strided(oT[HI:R, 0, 0:1], [[1, TOK]]), pO1[0:C, 0:TOK],
                                  cols[HI:R, j.t, BV:BV + 1], None, ALU.add).then_inc(oT1_done, 1)

            def sums(j, q):
                dve.wait_ge(exp_done, gv(j, 4, q + 1))
                e = strided(E[:, j.mod(2), 2 * q, 0, 0:1], [[HI, 2 * HEADS], [1, N]])
                dve.tensor_reduce(sm[:, 2 * HEADS * q:2 * HEADS * (q + 1)], e, AX.X, ALU.add)\
                   .then_inc(sum_done, 1)

            def inverse_sums(j, q):
                h = slice(2 * HEADS * q, 2 * HEADS * (q + 1))
                dve.wait_ge(sum_done, gv(j, 4, q + 1))
                dve.reciprocal(rs[:, j.mod(2), h], sm[:, h]).then_inc(rcp_done, 1)

            def normal1(j):
                t, s = j.t, PH[j.t]["shift"]
                dve.wait_ge(rs1_done, gv(j, 1, 1))

                def windows(p0, n, j0, c0, w):
                    src = [[WIN, n], [W, WIN], [1, w]]
                    return dve.tensor_tensor(
                        strided(xn1[:, p0, 0, j0:j0 + 1], [[N, n], [WIN, WIN], [1, w]]),
                        strided(pA0[0:R, c0:c0 + 1], src), strided(rs1[:, c0:c0 + 1], src), ALU.mult)

                if s:
                    windows(0, P - 1, 0, s, WIN)
                    windows(P - 1, 1, 0, W - WIN + s, WIN - s)
                    ins = windows(P - 1, 1, WIN - s, 0, s)
                else:
                    ins = windows(0, P, 0, 0, WIN)
                ins.then_inc(xn1_done, 1)

            def residual1(j):
                t, s = j.t, PH[j.t]["shift"]
                dve.wait_ge(proj_mm, gv(j, 1, 1))
                if not j.before(2):
                    dve.wait_ge(x2_done, gv(j, 1, -1))
                to = x1[:, j.mod(2)]
                y = pD0[0:R, 0:TOK].rearrange("p (r c) -> p r c", r=WIN)
                x = xin[:, j.mod(XB)].rearrange("p (r c) -> p r c", r=WIN)
                bp = cols[:, t, BP:BP + 1]
                ins = dve.scalar_tensor_tensor(to[:, :, s:W], y[:, :, 0:W - s], bp, x[:, :, s:W], ALU.add, ALU.add)
                if s:
                    ins = dve.scalar_tensor_tensor(to[:, :, 0:s], y[:, :, W - s:W], bp, x[:, :, 0:s],
                                                   ALU.add, ALU.add)
                ins.then_inc(x1_done, 1)

            def normal2(j):
                dve.wait_ge(rs2_done, gv(j, 1, 1))
                dve.tensor_tensor(xn2[:, :], pD1[0:R, 0:TOK], rs2[:, :], ALU.mult).then_inc(xn2_done, 1)

            def residual2(j):
                t = j.t
                b = j.mod(2)
                dve.wait_ge(fc2_mm, gv(j, 1, 1))
                if not j.before(2):
                    dve.wait_ge(out_st[b], j.uses(2) * 32 + t * 32 * STEPS // 2)
                dve.wait_ge(x1_done, gv(j, 1, 1))
                dve.scalar_tensor_tensor(xout[:, b], pD1[0:R, 0:TOK], cols[:, t, B2:B2 + 1],
                                         x1[:, j.mod(2)].rearrange("p r c -> p (r c)"), ALU.add, ALU.add)\
                   .then_inc(x2_done, 1)

            def high(j, ready, x, hi, done):
                dve.wait_ge(ready, gv(j, 1, 1))
                dve.tensor_copy(hi[:, :], x).then_inc(done, 1)

            def high_x(j):
                dve.wait_ge(xin_in[j.mod(XB)], j.uses(XB) * 32 + 32 + j.t * 32 * STEPS // XB)
                if not j.before(1):
                    dve.wait_ge(ctr1_mm, gv(j, 1, 0))
                dve.tensor_copy(x_hi[:, :], xin[:, j.mod(XB)]).then_inc(x_hi_done, 1)

            def parts(j, ready, x, hi, lo, hi_done, done):
                high(j, ready, x, hi, hi_done)
                dve.wait_ge(hi_done, gv(j, 1, 1))
                dve.tensor_tensor(lo[:, :], x, hi[:, :].bitcast(fp32), ALU.subtract).then_inc(done, 1)

            def iteration(a, b, c, d, e):
                for p in range(P):
                    if b:
                        scores(b, p)
                    if p == 0:
                        if a and a.before(1):
                            high_x(a)
                        if c:
                            less_maxima(c, 3)
                            inverse_sums(c, 2)
                        if d:
                            evac_o(d)
                    if p == 1:
                        if b:
                            maxima(b, 0)
                        if c:
                            sums(c, 3)
                        if b:
                            less_maxima(b, 0)
                        if c:
                            inverse_sums(c, 3)
                    if p == 2:
                        if e:
                            normal2(e)
                            parts(e, xn2_done, xn2[:, :], xn2_hi, xn2_lo, xn2_hi_done, xn2_lo_done)
                    if p == 3:
                        if b:
                            maxima(b, 1)
                            sums(b, 0)
                    if p == 4:
                        if b:
                            less_maxima(b, 1)
                            inverse_sums(b, 0)
                        if a:
                            normal1(a)
                            parts(a, xn1_done, flat(xn1), xn1_hi, xn1_lo, xn1_hi_done, xn1_lo_done)
                    if p == 5:
                        if b:
                            maxima(b, 2)
                            sums(b, 1)
                            less_maxima(b, 2)
                            inverse_sums(b, 1)
                    if p == 6:
                        if d:
                            residual1(d)
                            high(d, x1_done, x1[:, d.mod(2)].rearrange("p r c -> p (r c)"), x1_hi, x1_hi_done)
                    if p == 7:
                        if e:
                            residual2(e)
                        if b:
                            maxima(b, 3)
                        if a and not a.last():
                            high_x(a.next())
                        if b:
                            sums(b, 2)

            sweep(dve, iteration)

            def gather_tm(j):
                b = j.mod(4)
                dve.wait_ge(tr2_done, j.val(1, 1))
                if not j.before(4):
                    dve.wait_ge(to_out[b], 16 * j.uses(4))
                src = strided(bank[j.mod(2)][0:TP, 0:1], [[R, TK], [HI, 2], [1, C]])
                dst = strided(tm[:, b, 0, 0:1], [[C, TK], [TK * C, 2], [1, C]])
                dve.tensor_copy(dst, src).then_inc(to_done, 1)

            for c in range(UN):
                gather_tm(Step(0, c))
            with dve.Fori(1, STEPS // UN) as u:
                for c in range(UN):
                    gather_tm(Step(u, c))

        @block.tensor
        def _(pe):
            mm = pe.matmul
            pe.wait_ge(const_in, 16 * len(consts))
            def transpose_x(j):
                b = j.mod(4)
                pe.wait_ge(tz_done, j.val(1, 1))
                if not j.before(2):
                    pe.wait_ge(cm_done, j.val(1, -1))
                for k in range(TK):
                    last = pe.transpose(bank[j.mod(2)][0:R, k * TP:(k + 1) * TP], tz[:, b, k, 0:R], ident[0:TP, 0:TP])
                last.then_inc(tr_done, 1)

            for c in range(UN):
                transpose_x(Step(0, c))
            with pe.Fori(1, STEPS // UN) as u:
                for c in range(UN):
                    transpose_x(Step(u, c))
            pe.wait_ge(cm_done, STEPS)

            pe.wait_ge(par_in, 16 * len(par))
            for k, (_, ts_) in enumerate(TABLES):
                pe.wait_ge(onehot, k + 1)
                for t in ts_:
                    for r in (0, HI):
                        for m in range(N):
                            o = bank[2 + t][r:r + N, HEADS * m:HEADS * (m + 1)]
                            mm(o, strided(oh_lo[:, m:m + 1], [[N, N]]), tab[:, t, 0], start=True, stop=False)
                            last = mm(o, strided(oh_hi[:, m:m + 1], [[N, N]]), tab[:, t, 1], start=False, stop=True)
                    last.then_inc(tab_mm, 1)
            for t in range(NPH):
                o = 8 * t
                be1, be2 = cols[:, t, BE1:BE1 + 1], cols[:, t, BE2:BE2 + 1]
                for i, w in enumerate((wq, wk, wvr)):
                    mm(bank[6][0:R, o + i:o + i + 1], w[:, t], be1, start=True, stop=True)
                for k in range(3):
                    last = mm(bank[6][:, o + 3 + k:o + 4 + k], w1[:, t, k], be2, start=True, stop=True)
                last.then_inc(bias_mm, 1)

            def transposes(j, p):
                if p % 2 == 0:
                    pe.wait_ge(norm_done, gv(j, 4, p // 2 + 1))
                if not (j.before(1) and p == 0):
                    pe.wait_ge(et_done, gv(j, P, p))
                for k in range(HP):
                    last = pe.transpose(pT[0:M2, k * M2:(k + 1) * M2],
                                        strided(E[:, j.mod(2), p, 2 * k, 0:1], [[1, M2]]), ident[0:M2, 0:M2])
                last.then_inc(tr_mm, 1)

            def scores(j, p):
                if p == 0:
                    pe.wait_ge(q_done, gv(j, 1, 1))
                if p % (P // 2) == 0:
                    pe.wait_ge(kbd_done, gv(j, 2, 1 + 2 * p // P))
                if not (j.before(1) and p == 0):
                    pe.wait_ge(s_done, gv(j, P, p))
                mm(pS[0:M2, 0:HN], Qbd[:, j.mod(2), p, 0:M2],
                   strided(Kbd[:, j.mod(2), p, 0, 0:1], [[1, HN]]), start=True, stop=True).then_inc(s_mm, 1)

            def values(j, p):
                pe.wait_ge(et_done, gv(j, P, p + 1))
                if p == 0:
                    pe.wait_ge(v_done, gv(j, 2, 2))
                    if not j.before(1):
                        pe.wait_ge(oT_done, gv(j, 1, 0))
                        pe.wait_ge(oT1_done, gv(j, 1, 0))
                for w in range(2):
                    for k in range(HP):
                        last = mm(pO[w][0:C, N * p:N * (p + 1)],
                                  V2[:, j.mod(4), 2 * p + w, C * k:C * (k + 1)],
                                  ET[:, p % 2, k, HI * w:HI * w + N], start=(k == 0), stop=(k == HP - 1))
                last.then_inc(pv_mm, 1)

            def one_pass(to, w, x, start, stop):
                return mm(to, w, x, start=start, stop=stop)

            def split_product(to, w, hi, lo, hi_done, lo_done, j):
                pe.wait_ge(hi_done, gv(j, 1, 1))
                one_pass(to, w[:, :], hi[:, :], True, False)
                pe.wait_ge(lo_done, gv(j, 1, 1))
                return one_pass(to, w[:, :], lo[:, :], False, True)

            def center1(j):
                if not j.before(1):
                    pe.wait_ge(v_done, gv(j, 2, 0))
                split_product(pA0[0:R, 0:TOK], center_hi, x_hi, x_lo, x_hi_done, x_lo_done, j).then_inc(ctr1_mm, 1)

            def var1(j):
                pe.wait_ge(sq1_done, gv(j, 1, 1))
                mm(pA1[0:R, 0:TOK], ones[:, :], sq1[:, :], start=True, stop=True).then_inc(var1_mm, 1)

            def query_key(j):
                t = j.t
                pe.wait_ge(xn1_hi_done, gv(j, 1, 1))
                for to, hi, lo in ((pA1, wq_hi, wq_lo), (pA0, wk_hi, wk_lo)):
                    one_pass(to[0:R, 0:TOK], hi[:, t], xn1_hi[:, :], True, False)
                    one_pass(to[0:R, 0:TOK], lo[:, t], xn1_hi[:, :], False, False)
                pe.wait_ge(xn1_lo_done, gv(j, 1, 1))
                one_pass(pA1[0:R, 0:TOK], wq_hi[:, t], xn1_lo[:, :], False, True).then_inc(q_mm, 1)
                one_pass(pA0[0:R, 0:TOK], wk_hi[:, t], xn1_lo[:, :], False, True).then_inc(k_mm, 1)

            def value(j, half):
                t = j.t
                pe.wait_ge((q_done, kT_done)[half], gv(j, 1, 1))
                for i in range(P // 2):
                    x = strided(xn1[:, half * P // 2 + i, 0, 0:1], [[1, N]])
                    last = mm((pA1, pA0)[half][0:N, 2 * C * i:2 * C * (i + 1)], x,
                              wv[:, t], start=True, stop=True)
                last.then_inc(v_mm, 1)

            def project(j):
                t = j.t
                pe.wait_ge(oT_done, gv(j, 1, 1))
                pe.wait_ge(oT1_done, gv(j, 1, 1))
                if not j.before(1):
                    pe.wait_ge(gelu_done, gv(j, 3, 0))
                rolled = strided(oT[:, 0, 0:1], [[WIN, WIN], [N, P], [1, WIN]])
                mm(pD0[0:R, 0:TOK], wp[:, t], rolled, start=True, stop=True).then_inc(proj_mm, 1)

            def center2(j):
                pe.wait_ge(x1_done, gv(j, 1, 1))
                if not j.before(1):
                    pe.wait_ge(x2_done, gv(j, 1, 0))
                split_product(pD1[0:R, 0:TOK], center_hi, x1_hi, x1_lo, x1_hi_done, x1_lo_done, j).then_inc(ctr2_mm, 1)

            def var2(j):
                pe.wait_ge(sq2_done, gv(j, 1, 1))
                mm(pD0[0:R, 0:TOK], ones[:, :], sq2[:, :], start=True, stop=True).then_inc(var2_mm, 1)

            def up(j, chunks):
                t = j.t
                pe.wait_ge(xn2_hi_done, gv(j, 1, 1))
                to = [(pD0, pD1, pD0)[k][:, 0:TOK] for k in range(3)]
                if 2 in chunks:
                    pe.wait_ge(gelu_done, gv(j, 3, 1))
                for k in chunks:
                    one_pass(to[k], w1_hi[:, t, k], xn2_hi[:, :], True, False)
                    one_pass(to[k], w1_lo[:, t, k], xn2_hi[:, :], False, False)
                pe.wait_ge(xn2_lo_done, gv(j, 1, 1))
                for k in chunks:
                    one_pass(to[k], w1_hi[:, t, k], xn2_lo[:, :], False, True).then_inc(fc1_mm, 1)

            def down(j):
                t = j.t
                for k in range(3):
                    pe.wait_ge(gelu_done, gv(j, 3, max(k, 1) + 1))
                    last = mm(pD1[0:R, 0:TOK], w2[:, t, k], hT[:, k], start=(k == 0), stop=(k == 2))
                last.then_inc(fc2_mm, 1)

            def iteration(a, b, c, d, e):
                for p in range(P):
                    if c:
                        transposes(c, p)
                    if b:
                        scores(b, p)
                    if p == 1:
                        if a:
                            center1(a)
                        if e:
                            var2(e)
                    if p == 2:
                        if a:
                            var1(a)
                    if p == 4:
                        if e:
                            up(e, (2,))
                    if p == 5:
                        if d:
                            project(d)
                    if p == 6:
                        if e:
                            down(e)
                    if p == 7:
                        if a:
                            value(a, 0)
                            value(a, 1)
                    if c and p:
                        values(c, p - 1)
                    if p == 0 and d:
                        values(d, P - 1)
                    if p == 0 and e:
                        center2(e)
                    if p == 3 and e:
                        up(e, (0, 1))
                    if p == 5 and a:
                        query_key(a)

            sweep(pe, iteration)

            pe.wait_ge(x2_done, NPH * STEPS)

            def transpose_out(j):
                b = j.mod(4)
                pe.wait_ge(cm_in[b], 16 * j.uses(4) + 16)
                if not j.before(2):
                    pe.wait_ge(to_done, j.val(1, -1))
                for k in range(TK):
                    last = pe.transpose(bank[j.mod(2)][0:TP, k * R:(k + 1) * R],
                                        strided(cm[:, b, k:k + 1], [[TK, TP]]), ident[0:R, 0:R])
                last.then_inc(tr2_done, 1)

            for c in range(UN):
                transpose_out(Step(0, c))
            with pe.Fori(1, STEPS // UN) as u:
                for c in range(UN):
                    transpose_out(Step(u, c))


def constants():
    eye = np.eye(128, dtype=np.float32)
    center = np.zeros((R, R), np.float32)
    ones = np.zeros((R, R), np.float32)
    headmask = np.zeros((R, HEADS), np.float32)
    for r in (0, HI):
        ones[r:r + C, r:r + C] = 1.0
        center[r:r + C, r:r + C] = C * np.eye(C) - 1.0
        for h in range(HEADS):
            headmask[r + D * h:r + D * (h + 1), h] = 1.0
    kcol = np.stack([np.arange(128), np.arange(128) + 128], 1).astype(np.float32)
    i, j = np.divmod(np.arange(N), WIN)
    col = (j[:, None] < WIN - SHIFT) != (j[None, :] < WIN - SHIFT)
    row = (i[:, None] < WIN - SHIFT) != (i[None, :] < WIN - SHIFT)
    regions = np.stack([col, row, col | row], 1).astype(np.float32)
    rel = ((i[:, None] - i[None, :] + WIN - 1) * (2 * WIN - 1) + j[:, None] - j[None, :] + WIN - 1)
    return dict(ident=eye, center=center, ones=ones, headmask=headmask, kcol=kcol, regions=regions,
                rel_const=rel.reshape(-1).astype(np.int32))


def kernel(**inputs):
    import concourse.bacc as bacc
    from concourse.bass_utils import run_bass_kernel_spmd

    nc = bacc.Bacc("TRN2", target_bir_lowering=False, num_devices=1)
    arrays, aps = {}, {}
    for name, a in {**inputs, **constants()}.items():
        a = np.ascontiguousarray(a)
        arrays[f"in_{name}"] = a
        aps[name] = nc.dram_tensor(f"in_{name}", a.shape, mybir.dt.from_np(a.dtype), kind="ExternalInput").ap()
    out = nc.dram_tensor("out", (B, H, W, C), mybir.dt.float32, kind="ExternalOutput").ap()
    build(nc, aps, out)
    r = run_bass_kernel_spmd(nc, [arrays], core_ids=[0])
    return r.results[0]["out"]
```
